# Optimizing a Trainium2 kernel written in Bass

```python
import numpy as np
import jax
import jax.numpy as jnp

def _softmax(x, axis=-1):
    return jax.nn.softmax(x, axis=axis)

def _gelu(x):
    return jax.nn.gelu(x, approximate=True)

def _silu(x):
    return jax.nn.silu(x)

def _sigmoid(x):
    return jax.nn.sigmoid(x)

def _layernorm(x, axis=-1, eps=1e-05):
    m = jnp.mean(x, axis=axis, keepdims=True)
    v = jnp.var(x, axis=axis, keepdims=True)
    return (x - m) / jnp.sqrt(v + eps)

def _scatter_add(tgt, idx, src, axis=0):
    return tgt.at[idx].add(src)

def _segment_sum(src, seg, n):
    return jax.ops.segment_sum(src, seg, n)
kernel_name = 'mk_cond_resid_d2_seqx_r2_b4e9fa'

def setup_inputs(seed: int=0):
    np.random.seed(seed)
    _w = jnp.asarray

    def _rec_inputs():
        import jax
        import jax.numpy as jnp
        _rk = jax.random.key(seed)
        x = -0.0002928 + 1 * jax.random.normal(jax.random.fold_in(_rk, 1), (8, 512, 512), jnp.float32)
        _lenS = 512 - jax.random.randint(jax.random.fold_in(_rk, 7), (8,), 0, max(1, 512 // 4) + 1, jnp.int32)
        _lenS2 = 512 - jax.random.randint(jax.random.fold_in(_rk, 8), (8,), 0, max(1, 512 // 4) + 1, jnp.int32)
        cond_256 = -0.106481 + 1.03144 * jax.random.normal(jax.random.fold_in(_rk, 12), (8, 128), jnp.float32)
        _validS = jnp.arange(512)[None, :] < _lenS[:, None]
        _validS2 = jnp.arange(512)[None, :] < _lenS2[:, None]
        _causal = jnp.tril(jnp.ones((512, 512), dtype=bool))
        mask_SxS_bk1 = jnp.broadcast_to(_validS[0:1, :], (512, 512))
        return (x, cond_256, mask_SxS_bk1)
    x, cond_256, mask_SxS_bk1 = _rec_inputs()

    def _L0_cond_setup():
        import jax, jax.numpy as jnp
        import numpy as np
        EPS = 1e-06
        key = jax.random.key(seed)
        ks = jax.random.split(key, 8)
        B, S, E, C = (2, 1024, 512, 128)
        x = jax.random.normal(ks[0], (B, S, E), dtype=jnp.float32)
        mask = jnp.triu(jnp.ones((S, S), dtype=bool), k=1)
        conditioning = jax.random.normal(ks[1], (B, C), dtype=jnp.float32)
        sc = 1.0 / np.sqrt(E)
        Wq = jax.random.normal(ks[2], (E, E), dtype=jnp.float32) * sc
        Wk = jax.random.normal(ks[3], (E, E), dtype=jnp.float32) * sc
        Wv = jax.random.normal(ks[4], (E, E), dtype=jnp.float32) * sc
        Wo = jax.random.normal(ks[5], (E, E), dtype=jnp.float32) * sc
        rms_scale = jnp.ones((E,), dtype=jnp.float32)
        Wc = jax.random.normal(ks[6], (2 * E, C), dtype=jnp.float32) * 0.02
        bc = jax.random.normal(ks[7], (2 * E,), dtype=jnp.float32) * 0.02
        return {'x': x, 'mask': mask, 'conditioning': conditioning, 'Wq': Wq, 'Wk': Wk, 'Wv': Wv, 'Wo': Wo, 'rms_scale': rms_scale, 'Wc': Wc, 'bc': bc}
    _L0_cond_all = _L0_cond_setup()
    _L0_cond_in = {k: v for k, v in _L0_cond_all.items() if k in ('Wq', 'Wk', 'Wv', 'Wo', 'rms_scale', 'Wc', 'bc')}
    del _L0_cond_all

    def _L1_cond_setup():
        import jax, jax.numpy as jnp
        import numpy as np
        EPS = 1e-08

        def hamilton(q1, q2):
            w1, x1, y1, z1 = (q1[..., i, :] for i in range(4))
            w2, x2, y2, z2 = (q2[..., i, :] for i in range(4))
            w = w1 * w2 - x1 * x2 - y1 * y2 - z1 * z2
            x = w1 * x2 + x1 * w2 + y1 * z2 - z1 * y2
            y = w1 * y2 - x1 * z2 + y1 * w2 + z1 * x2
            z = w1 * z2 + x1 * y2 - y1 * x2 + z1 * w2
            return jnp.stack([w, x, y, z], axis=-2)

        def _normalize(q):
            return q / jnp.sqrt(jnp.sum(q * q, axis=0, keepdims=True) + EPS)
        key = jax.random.key(seed)
        k1, k2, k3, k4 = jax.random.split(key, 4)
        B, T, d_model = (4, 2048, 512)
        quat_dim = d_model // 4
        x = jax.random.normal(k1, (B, T, d_model), dtype=jnp.float32)
        q_left = jax.random.normal(k2, (4, quat_dim), dtype=jnp.float32)
        q_right = jax.random.normal(k3, (4, quat_dim), dtype=jnp.float32)
        spectral_gate = jax.random.uniform(k4, (1, 1, 1, quat_dim), dtype=jnp.float32)
        return {'x': x, 'q_left': q_left, 'q_right': q_right, 'spectral_gate': spectral_gate}
    _L1_cond_all = _L1_cond_setup()
    _L1_cond_in = {k: v for k, v in _L1_cond_all.items() if k in ('q_right', 'spectral_gate')}
    del _L1_cond_all
    return {'x': x, 'cond_256': cond_256, 'mask_SxS_bk1': mask_SxS_bk1, 'L0_cond_Wq': _L0_cond_in['Wq'], 'L0_cond_Wk': _L0_cond_in['Wk'], 'L0_cond_Wv': _L0_cond_in['Wv'], 'L0_cond_Wo': _L0_cond_in['Wo'], 'L0_cond_rms_scale': _L0_cond_in['rms_scale'], 'L0_cond_Wc': _L0_cond_in['Wc'], 'L0_cond_bc': _L0_cond_in['bc'], 'L1_cond_q_right': _L1_cond_in['q_right'], 'L1_cond_spectral_gate': _L1_cond_in['spectral_gate']}

def reference(x, cond_256, mask_SxS_bk1, L0_cond_Wq, L0_cond_Wk, L0_cond_Wv, L0_cond_Wo, L0_cond_rms_scale, L0_cond_Wc, L0_cond_bc, L1_cond_q_right, L1_cond_spectral_gate):
    import jax
    import jax.numpy as jnp

    def _L0_cond_ref(x, mask, conditioning, Wq, Wk, Wv, Wo, rms_scale, Wc, bc):
        import jax, jax.numpy as jnp
        import numpy as np
        EPS = 1e-06
        B, S, E = x.shape
        H = 16
        D = E // H
        scale = D ** (-0.5)

        def proj(W):
            return (x @ W.T).reshape(B, S, H, D).transpose(0, 2, 1, 3)
        q, k, v = (proj(Wq), proj(Wk), proj(Wv))
        scores = jnp.einsum('bhsd,bhtd->bhst', q, k) * scale
        scores = jnp.where(mask[None, None, :, :], -jnp.inf, scores)
        attn = jax.nn.softmax(scores, axis=-1)
        out = jnp.einsum('bhst,bhtd->bhsd', attn, v)
        out = out.transpose(0, 2, 1, 3).reshape(B, S, E)
        out = out @ Wo.T
        rms = jnp.sqrt(jnp.mean(out * out, axis=-1, keepdims=True) + EPS)
        xn = out / rms * rms_scale
        mod = jax.nn.silu(conditioning) @ Wc.T + bc
        shift, sc = jnp.split(mod, 2, axis=-1)
        xn = xn * (1.0 + sc[:, None, :]) + shift[:, None, :]
        return xn

    def _L1_cond_ref(x, q_left, q_right, spectral_gate):
        import jax, jax.numpy as jnp
        import numpy as np
        EPS = 1e-08

        def hamilton(q1, q2):
            w1, x1, y1, z1 = (q1[..., i, :] for i in range(4))
            w2, x2, y2, z2 = (q2[..., i, :] for i in range(4))
            w = w1 * w2 - x1 * x2 - y1 * y2 - z1 * z2
            x = w1 * x2 + x1 * w2 + y1 * z2 - z1 * y2
            y = w1 * y2 - x1 * z2 + y1 * w2 + z1 * x2
            z = w1 * z2 + x1 * y2 - y1 * x2 + z1 * w2
            return jnp.stack([w, x, y, z], axis=-2)

        def _normalize(q):
            return q / jnp.sqrt(jnp.sum(q * q, axis=0, keepdims=True) + EPS)
        B, T, d_model = x.shape
        quat_dim = d_model // 4
        x_quat = x.reshape(B, T, 4, quat_dim)
        x_spectral = jnp.fft.fft(x_quat, axis=1)
        x_filtered = jnp.fft.ifft(x_spectral * spectral_gate, axis=1).real.astype(x.dtype)
        q_left_n = _normalize(q_left)
        q_right_n = _normalize(q_right)
        conj_sign = jnp.array([1.0, -1.0, -1.0, -1.0], dtype=x.dtype)[:, None]
        q_right_conj = q_right_n * conj_sign
        x_right = hamilton(x_filtered, q_right_conj)
        x_rotated = hamilton(q_left_n, x_right)
        return x_rotated.reshape(B, T, d_model)
    x = x + _L0_cond_ref(x, mask_SxS_bk1, cond_256, L0_cond_Wq, L0_cond_Wk, L0_cond_Wv, L0_cond_Wo, L0_cond_rms_scale, L0_cond_Wc, L0_cond_bc)
    x = x + _L1_cond_ref(x, cond_256, L1_cond_q_right, L1_cond_spectral_gate)
    return x

_drawn_inputs = setup_inputs


def setup_inputs(seed=0):
    import zlib

    import numpy as np

    out = dict(_drawn_inputs(seed))
    spreads = {'L0_cond_rms_scale': (1.0, 0.2)}
    factors = {'L0_cond_bc': 2.863}
    for name, (base, spread) in spreads.items():
        noise = np.random.default_rng([zlib.crc32(name.encode()), seed]).standard_normal(out[name].shape)
        drawn = base * np.exp(spread * noise) if base else spread * noise
        out[name] = jnp.asarray(drawn.astype(out[name].dtype))
    for name, factor in factors.items():
        out[name] = (out[name] * factor).astype(out[name].dtype)
    return out
```

```python
from contextlib import ExitStack

import concourse.bass as bass
from concourse import mybir

ALU = mybir.AluOpType
ACT = mybir.ActivationFunctionType
AX_X = mybir.AxisListType.X
F32 = mybir.dt.float32
F32R = mybir.dt.float32r
BF16 = mybir.dt.bfloat16
U8 = mybir.dt.uint8

P = 128
B, S, E = 8, 512, 512
H, D = 16, 32
C = 128
KC = E // P
TC = S // P
HG = P // D
NG = H // HG
HALF = S // 2
STEPS = 2 * NG
TILES = 2 * HG
MASKED = 1e30
QSCALE = -float(D) ** -0.5
RMS_EPS, NORM_EPS = 1e-6, 1e-8


def f32(ap):
    return ap.bitcast(F32)


def projections(nc, xT, wT, scr, wo_hi, wo_lo, mask, condT, cond, wcT, bc, rms_scale, q_right, gate, mod_scr,
                mask_bias, rot, ident):
    with ExitStack() as ctx:
        def sb(name, shape, dt):
            return ctx.enter_context(nc.sbuf_tensor(name, shape, dt))

        def sem(name):
            return ctx.enter_context(nc.semaphore(name))

        w_raw = sb("w_raw", [P, 2, KC, E], F32)
        w_hi = [sb(f"w_hi_{n}", [P, KC, E], F32R) for n in "qkv"] + [wo_hi]
        w_lo = [sb(f"w_lo_{n}", [P, KC, E], F32R) for n in "qkv"] + [wo_lo]
        x_raw = sb("x_raw", [P, 2, KC, S], F32)
        x_hi = sb("x_hi", [P, 2, KC, S], F32R)
        x_lo = sb("x_lo", [P, 2, KC, S], F32R)
        qk_hi = sb("qk_hi", [P, 4, S], F32R)
        qk_lo = sb("qk_lo", [P, 4, S], F32R)
        v_out = sb("v_out", [P, 4, E], F32)
        proj = ctx.enter_context(nc.psum_tensor("proj", [P, 4, 512], F32))

        mask_words = sb("mask_words", [P, TC, S // 4], mybir.dt.int32)
        mask_u8 = mask_words[:, :, :].bitcast(U8)
        row_least = sb("row_least", [P, TC], F32)
        row_open = sb("row_open", [P, TC], F32)
        row_nan = sb("row_nan", [P, TC], F32)
        nan_part = sb("nan_part", [P, 1], F32)
        ones8 = sb("ones8", [P, B], F32)
        nan_all = sb("nan_all", [B, 1], F32)
        cT = sb("cT", [P, B], F32)
        c_sig = sb("c_sig", [P, B], F32)
        c_silu = sb("c_silu", [P, B], F32)
        wc = sb("wc", [P, 2 * E], F32)
        bc8 = sb("bc8", [B, 2 * E], F32)
        rms8 = sb("rms8", [B, E], F32)
        mod = sb("mod", [B, 2 * E], F32)
        quat = sb("quat", [P, 12, C], F32)
        square = sb("square", [P, 12, C], F32)
        neg_half = sb("neg_half", [P, 2, C], F32)
        gate_b = sb("gate_b", [P, C], F32)
        term = sb("term", [P, 4, 4, C], F32)
        left = w_raw[:, 0].rearrange("p k (i d) -> p k i d", i=4)
        right = w_raw[:, 1].rearrange("p k (j d) -> p k j d", j=4)
        mod_ps = ctx.enter_context(nc.psum_tensor("mod_ps", [P, 3, 512], F32))

        loaded = sem("loaded")
        pool_step, dve_step = sem("pool_step"), sem("dve_step")
        sig_exp, silu_ready = sem("sig_exp"), sem("silu_ready")
        nan_ready = sem("nan_ready")
        mod_matmul = sem("mod_matmul")
        mod_ready, mod_stored = sem("mod_ready"), sem("mod_stored")

        w_in = [sem(f"w_in{i}") for i in range(2)]
        x_in = [sem(f"x_in{i}") for i in range(2)]
        w_hi_ready, w_lo_ready = sem("w_hi_ready"), sem("w_lo_ready")
        x_hi_ready, x_lo_ready = sem("x_hi_ready"), sem("x_lo_ready")
        projected = sem("projected")
        v_copied = sem("v_copied")
        qk_hi_ready, qk_lo_ready = sem("qk_hi_ready"), sem("qk_lo_ready")
        v_stored = [sem(f"v_stored{i}") for i in range(4)]
        qk_stored = [sem(f"qk_stored{i}") for i in range(4)]

        VT, QKT = TC, 2 * NG
        TASKS = VT + QKT
        W_ORDER = (2, 0, 1, 3)
        LOADED = 16 * 8

        block = ctx.enter_context(nc.Block())

        @block.sync
        def _(sp):
            def load_x(b, p):
                sp.dma_start(x_raw[:, p], xT[b].rearrange("(k p) t -> p k t", p=P)).then_inc(x_in[p], 16)

            def load_w(n):
                sp.dma_start(w_raw[:, n % 2], wT[W_ORDER[n]].rearrange("(k p) e -> p k e", p=P)).then_inc(w_in[n % 2], 16)

            load_w(0)
            load_x(0, 0)
            load_w(1)
            sp.dma_start(mask_words[:, :, :], mask.rearrange("(c p) t -> p c t", p=P)).then_inc(loaded, 16)
            sp.dma_start(cT[:, :], condT).then_inc(loaded, 16)
            sp.dma_start(quat[:, 0:8, :], cond.partition_broadcast(P)).then_inc(loaded, 16)
            sp.dma_start(quat[:, 8:12, :], q_right.partition_broadcast(P)).then_inc(loaded, 16)
            sp.dma_start(gate_b[:, :], gate.partition_broadcast(P)).then_inc(loaded, 16)
            sp.dma_start(wc[:, :], wcT).then_inc(loaded, 16)
            sp.dma_start(bc8[:, :], bc.partition_broadcast(B)).then_inc(loaded, 16)
            sp.dma_start(rms8[:, :], rms_scale.partition_broadcast(B)).then_inc(loaded, 16)
            load_x(1, 1)
            for n in (2, 3):
                sp.wait_ge(w_lo_ready, n - 1)
                load_w(n)

            def store_v(b, c):
                sp.wait_ge(v_copied, VT * b + c + 1)
                sp.dma_start(scr["v"][b, c], v_out[:, c, :]).then_inc(v_stored[c], 16)

            def store_qk(b, which, g):
                j = g
                sp.wait_ge(qk_lo_ready, QKT * b + NG * which + g + 1)
                to = scr["qk"[which]][b * NG + g]
                sp.dma_start(to[0], f32(qk_hi[:, j, :])).then_inc(qk_stored[j], 16)
                sp.dma_start(to[1], f32(qk_lo[:, j, :])).then_inc(qk_stored[j], 16)

            def batch(b, p, more):
                for c in range(TC):
                    store_v(b, c)
                if more:
                    sp.wait_ge(x_lo_ready, b + 1)
                    load_x(b + 2, p)
                for which in range(2):
                    for g in range(NG):
                        store_qk(b, which, g)

            with sp.Fori(0, B - 3, 2) as b:
                batch(b, 0, True)
                batch(b + 1, 1, True)
            batch(B - 2, 0, False)
            batch(B - 1, 1, False)
            sp.wait_ge(mod_ready, 1)
            sp.dma_start(mod_scr, mod[:, :]).then_inc(mod_stored, 16)
            sp.wait_ge(mod_stored, 16)
            for j in range(4):
                sp.wait_ge(v_stored[j], 16 * B)
                sp.wait_ge(qk_stored[j], 16 * 4 * B)

        @block.scalar
        def _(act):
            def split_w(n):
                act.wait_ge(w_in[n % 2], 16 * (n // 2 + 1))
                act.activation(w_hi[W_ORDER[n]][:, :, :], w_raw[:, n % 2], ACT.Copy).then_inc(w_hi_ready, 1)

            def split_x(b, p):
                act.wait_ge(x_in[p], 8 * (b - p) + 16)
                if not (isinstance(b, int) and b < 2):
                    act.wait_ge(projected, TASKS * (b - 1))
                act.activation(x_hi[:, p], x_raw[:, p], ACT.Copy).then_inc(x_hi_ready, 1)

            def batch(b, p, more, first=False):
                for c in range(VT):
                    act.wait_ge(projected, TASKS * b + c + 1)
                    if not first:
                        act.wait_ge(v_stored[c], 16 * b)
                    act.activation(v_out[:, c, :], proj[:, c, :], ACT.Copy).then_inc(v_copied, 1)
                for m in range(QKT):
                    act.wait_ge(projected, TASKS * b + VT + m + 1)
                    if not (first and m < 4):
                        act.wait_ge(qk_stored[m % 4], 64 * b + 32 * (m // 4))
                    act.activation(qk_hi[:, m % 4, :], proj[:, m % 4, :], ACT.Copy,
                                   scale=QSCALE if m < NG else 1.0).then_inc(qk_hi_ready, 1)
                    if m == 1 and more:
                        split_x(b + 1, 1 - p)

            split_w(0)
            split_x(0, 0)
            for n in (1, 2, 3):
                split_w(n)
            act.wait_ge(loaded, LOADED)
            act.activation(c_sig[:, :], cT[:, :], ACT.Exp, scale=-1.0).then_inc(sig_exp, 1)
            batch(0, 0, True, first=True)
            with act.Fori(1, B - 2, 2) as b:
                batch(b, 1, True)
                batch(b + 1, 0, True)
            batch(B - 1, 1, False)

        @block.vector
        def _(dve):
            def split_w(n):
                dve.wait_ge(w_hi_ready, n + 1)
                dve.tensor_tensor(w_lo[W_ORDER[n]][:, :, :], w_raw[:, n % 2], f32(w_hi[W_ORDER[n]][:, :, :]),
                                  ALU.subtract).then_inc(w_lo_ready, 1)

            def split_x(b, p):
                dve.wait_ge(x_hi_ready, b + 1)
                dve.tensor_tensor(x_lo[:, p], x_raw[:, p], f32(x_hi[:, p]), ALU.subtract).then_inc(x_lo_ready, 1)

            def batch(b, p, more):
                for m in range(QKT):
                    dve.wait_ge(qk_hi_ready, QKT * b + m + 1)
                    dve.scalar_tensor_tensor(qk_lo[:, m % 4, :], proj[:, m % 4, :], QSCALE if m < NG else 1.0,
                                             f32(qk_hi[:, m % 4, :]), ALU.mult, ALU.subtract).then_inc(qk_lo_ready, 1)
                    if m == 1 and more:
                        split_x(b + 1, 1 - p)

            split_w(0)
            split_x(0, 0)
            for n in (1, 2, 3):
                split_w(n)

            done = [0]

            def link(ins):
                done[0] += 1
                ins.then_inc(dve_step, 1)
                dve.wait_ge(dve_step, done[0])

            dve.wait_ge(loaded, LOADED)
            link(dve.tensor_scalar(mask_bias[:, :, :], mask_u8, MASKED, None, ALU.mult))
            link(dve.tensor_reduce(row_least[:, :], mask_bias[:, :, :], AX_X, ALU.min))
            link(dve.tensor_scalar(row_open[:, :], row_least[:, :], MASKED / 2, None, ALU.is_lt))
            link(dve.reciprocal(row_nan[:, :], row_open[:, :]))
            link(dve.tensor_scalar(row_nan[:, :], row_nan[:, :], 0.0, None, ALU.mult))
            dve.tensor_reduce(nan_part[:, :], row_nan[:, :], AX_X, ALU.add).then_inc(nan_ready, 1)
            dve.wait_ge(sig_exp, 1)
            link(dve.tensor_scalar(c_sig[:, :], c_sig[:, :], 1.0, None, ALU.add))
            link(dve.reciprocal(c_sig[:, :], c_sig[:, :]))
            dve.tensor_tensor(c_silu[:, :], cT[:, :], c_sig[:, :], ALU.mult).then_inc(silu_ready, 1)

            with dve.Fori(0, B - 3, 2) as b:
                batch(b, 0, True)
                batch(b + 1, 1, True)
            dve.wait_ge(mod_matmul, 3)
            link(dve.tensor_copy(nan_all[:, :], mod_ps[0:B, 2, 0:1]))
            link(dve.scalar_tensor_tensor(mod[:, 0:E], mod_ps[0:B, 0, :], nan_all[:, 0:1], bc8[:, 0:E],
                                          ALU.add, ALU.add))
            link(dve.tensor_tensor(mod[:, E:], mod_ps[0:B, 1, :], bc8[:, E:], ALU.add))
            dve.scalar_tensor_tensor(mod[:, E:], mod[:, E:], 1.0, rms8[:, :], ALU.add, ALU.mult).then_inc(mod_ready, 1)
            batch(B - 2, 0, True)
            batch(B - 1, 1, False)

        @block.tensor
        def _(pe):
            def passes(out, hi, lo, other_hi, other_lo):
                for k in range(KC):
                    pe.matmul(out, hi(k), other_hi(k), start=(k == 0), stop=False)
                    pe.matmul(out, hi(k), other_lo(k), start=False, stop=False)
                    last = pe.matmul(out, lo(k), other_hi(k), start=False, stop=(k == KC - 1))
                last.then_inc(projected, 1)

            def batch(b, p, first=False):
                for c in range(VT):
                    if c == 0:
                        pe.wait_ge(x_lo_ready, b + 1)
                    if first:
                        pe.wait_ge(w_lo_ready, 1)
                    else:
                        pe.wait_ge(qk_lo_ready, QKT * b - 4 + c + 1)
                    t = slice(c * P, (c + 1) * P)
                    passes(proj[:, c, :], lambda k: x_hi[:, p, k, t], lambda k: x_lo[:, p, k, t],
                           lambda k: w_hi[2][:, k, :], lambda k: w_lo[2][:, k, :])
                for m in range(QKT):
                    if m < 4:
                        pe.wait_ge(v_copied, VT * b + m + 1)
                    else:
                        pe.wait_ge(qk_lo_ready, QKT * b + m - 3)
                    w = m // NG
                    if first and m % NG == 0:
                        pe.wait_ge(w_lo_ready, 2 + w)
                    e = slice((m % NG) * P, (m % NG + 1) * P)
                    passes(proj[:, m % 4, :], lambda k: w_hi[w][:, k, e], lambda k: w_lo[w][:, k, e],
                           lambda k: x_hi[:, p, k, :], lambda k: x_lo[:, p, k, :])

            batch(0, 0, first=True)
            pe.wait_ge(silu_ready, 1)
            pe.wait_ge(nan_ready, 2)
            for h in range(2):
                pe.matmul(mod_ps[0:B, h, :], c_silu[:, :], wc[:, h * E:(h + 1) * E],
                          start=True, stop=True).then_inc(mod_matmul, 1)
            pe.matmul(mod_ps[0:B, 2, 0:1], ones8[:, :], nan_part[:, :], start=True, stop=True).then_inc(mod_matmul, 1)
            with pe.Fori(1, B - 2, 2) as b:
                batch(b, 1)
                batch(b + 1, 0)
            batch(B - 1, 1)

        @block.gpsimd
        def _(pool):
            done = [0]

            def link(ins):
                done[0] += 1
                ins.then_inc(pool_step, 1)
                pool.wait_ge(pool_step, done[0])

            pool.memset(ones8[:, :], 1.0).then_inc(nan_ready, 1)
            pool.memset(neg_half[:, :, :], -0.5)
            link(pool.memset(ident[:, :], 0.0))
            link(pool.affine_select(out=ident[:, :], in_=ident[:, :], compare_op=ALU.not_equal, fill=1.0,
                                    base=0, pattern=[[-1, P]], channel_multiplier=1))
            pool.wait_ge(loaded, LOADED)
            link(pool.tensor_tensor(square[:, :, :], quat[:, :, :], quat[:, :, :], ALU.mult))
            link(pool.tensor_tensor(square[:, 0:4, :], square[:, 0:4, :], square[:, 4:8, :], ALU.add))
            pool.tensor_tensor(square[:, 4:6, :], square[:, 0:2, :], square[:, 2:4, :], ALU.add)
            link(pool.tensor_tensor(square[:, 6:8, :], square[:, 8:10, :], square[:, 10:12, :], ALU.add))
            sums = square[:, 4:8, :].rearrange("p (q h) d -> p q h d", h=2)
            link(pool.tensor_tensor(square[:, 0:2, :], sums[:, :, 0, :], sums[:, :, 1, :], ALU.add))
            link(pool.tensor_scalar(square[:, 0:2, :], square[:, 0:2, :], 1.0, NORM_EPS, ALU.mult, ALU.add))
            link(pool.tensor_tensor(square[:, 2:4, :], square[:, 0:2, :], neg_half[:, :, :], ALU.pow))
            pool.tensor_tensor(quat[:, 0:4, :], quat[:, 0:4, :],
                               square[:, 2, :].unsqueeze(1).to_broadcast([P, 4, C]), ALU.mult)
            link(pool.tensor_tensor(square[:, 8, :], square[:, 3, :], gate_b[:, :], ALU.mult))
            link(pool.tensor_tensor(quat[:, 8:12, :], quat[:, 8:12, :],
                                    square[:, 8, :].unsqueeze(1).to_broadcast([P, 4, C]), ALU.mult))
            by_left = [[(0, 1), (1, -1), (2, -1), (3, -1)], [(1, 1), (0, 1), (3, -1), (2, 1)],
                       [(2, 1), (3, 1), (0, 1), (1, -1)], [(3, 1), (2, -1), (1, 1), (0, 1)]]
            by_right = [[(0, 1), (1, 1), (2, 1), (3, 1)], [(1, -1), (0, 1), (3, -1), (2, 1)],
                        [(2, -1), (3, 1), (0, 1), (1, -1)], [(3, -1), (2, -1), (1, 1), (0, 1)]]
            pool.wait_ge(w_lo_ready, 4)
            for i in range(4):
                for k in range(4):
                    q, sign = by_left[i][k]
                    pool.tensor_scalar(left[:, k, i, :], quat[:, q, :], float(sign), 0.0, ALU.mult, ALU.add)
            for k in range(4):
                for j in range(4):
                    q, sign = by_right[k][j]
                    last = pool.tensor_scalar(right[:, k, j, :], quat[:, 8 + q, :], float(sign), 0.0, ALU.mult, ALU.add)
            link(last)

            for k in range(4):
                to = rot if k == 0 else term
                for j in range(4):
                    last = pool.tensor_tensor(to[:, j], left[:, k], right[:, k, j, :].unsqueeze(1).to_broadcast([P, 4, C]),
                                              ALU.mult)
                link(last)
                if k > 0:
                    link(pool.tensor_tensor(rot[:, :, :, :], rot[:, :, :, :], term[:, :, :, :], ALU.add))
            for i in range(4):
                link(pool.tensor_scalar(rot[:, i, i, :], rot[:, i, i, :], 1.0, 1.0, ALU.mult, ALU.add))


def attention(nc, x, scr, mod_scr, out, mask_bias, rot, ident, wo_hi, wo_lo):
    with ExitStack() as ctx:
        def sb(name, shape, dt=F32):
            return ctx.enter_context(nc.sbuf_tensor(name, shape, dt))

        def ps(name, shape):
            return ctx.enter_context(nc.psum_tensor(name, shape, F32))

        def sem(name):
            return ctx.enter_context(nc.semaphore(name))

        q_rows = sb("q_rows", [P, 2, HG, S], F32R)
        k_rows = sb("k_rows", [P, 2, HG, S], F32R)
        v_sb = sb("v_sb", [P, 2, TC, E], F32)
        probs = sb("probs", [P, 2, TILES, S])
        den = sb("den", [P, 2, TILES])
        least = sb("least", [P, 2, TILES])
        inv_sum = sb("inv_sum", [P, 2, HG])
        inv_den = sb("inv_den", [P, 2, HG, D])
        scale_T = sb("scale_T", [P, HALF])
        probs_T = sb("probs_T", [P, 2, HG, TC, HALF])
        o_T = sb("o_T", [P, 2, HALF])
        o_hi = sb("o_hi", [P, 2, NG, S], F32R)
        o_lo = sb("o_lo", [P, 2, NG, S], F32R)
        mod = sb("mod_b", [P, 2, 2 * E])
        x_s = sb("x_s", [P, 2, E])
        scaled = sb("scaled", [P, E])
        junk = sb("junk", [P, E])
        sum_sq = sb("sum_sq", [P, 2])
        mean_sq = sb("mean_sq", [P, 2])
        rstd = sb("rstd", [P, 2])
        neg_half = sb("neg_half2", [P, 1])
        mix = sb("mix", [P, 4, E])
        acc = sb("acc", [P, 2, E])

        score_ps = ps("score_ps", [P, 4, 512])
        prob_ps = ps("prob_ps", [P, 2, 512])
        out_ps = ps("out_ps", [P, 2, HALF])
        value_ps, scale_ps = out_ps[:, 0, :], out_ps[:, 1, :]
        y_ps = ps("y_ps", [P, 512])

        q_in = [sem(f"q_in{i}") for i in range(2)]
        k_in = [sem(f"k_in{i}") for i in range(2)]
        v_in = [sem(f"v_in{i}") for i in range(2)]
        mod_in = [sem(f"mod_in{i}") for i in range(2)]
        x_in = [sem(f"xc_in{i}") for i in range(2)]
        stored = [sem(f"stored{i}") for i in range(2)]
        scores = sem("scores")
        masked = sem("masked")
        exped = sem("exped")
        inv_ready = sem("inv_ready2")
        inverted = sem("inverted")
        turned = sem("turned")
        out_act, out_dve = sem("out_act"), sem("out_dve")
        scale_turned = sem("scale_turned")
        scale_out = sem("scale_out")
        valued = sem("valued")
        o_scaled = sem("o_scaled")
        o_hi_ready, o_ready = sem("o_hi_ready"), sem("o_ready")
        y_ready = sem("y_ready")
        squared = sem("squared")
        mean_ready, rstd_ready = sem("mean_ready"), sem("rstd_ready")
        scaled_ready = sem("scaled_ready")
        shifted = sem("shifted")
        summed = sem("summed")
        half_set = sem("half_set")
        passed = sem("passed")
        mixing = sem("mixing")
        paired = sem("paired")
        rotated = sem("rotated")

        SCORE_AHEAD, MASK_AHEAD = 3, 2
        BY_ACT = (1, 3, 5, 7)
        BY_DVE = tuple(r for r in range(TILES) if r not in BY_ACT)

        def moved_out(eng, n, r):
            if r in BY_ACT:
                eng.wait_ge(out_act, len(BY_ACT) * n + BY_ACT.index(r) + 1)
            else:
                eng.wait_ge(out_dve, len(BY_DVE) * n + BY_DVE.index(r) + 1)

        def take_waits(eng):
            eng.sem_inc(passed, 1)

        def known(v, least_value):
            return isinstance(v, int) and v < least_value

        def tile_ahead(b, s, r, last):
            s, r = s + 1 + r // TILES, r % TILES
            if s < STEPS:
                return b, s, r
            return None if last else (b + 1, s - STEPS, r)

        def chunk_before(b, p, s):
            if s % 2 or known(b, 1) or (s == 0 and known(b, 2)):
                return None
            return (b - 1, 1 - p, s // 2 - 1) if s else (b - 2, p, TC - 1)

        block = ctx.enter_context(nc.Block())

        @block.sync
        def _(sp):
            def load_unit(u, g):
                p = g % 2
                if not known(u, 2):
                    sp.wait_ge(scores, TILES * 2 * (u - 1))
                for r in range(4):
                    rows = slice(r * D, (r + 1) * D)
                    sp.dma_start(f32(q_rows[rows, p]),
                                 scr["q"][u, r % 2].rearrange("(i d) t -> d i t", d=D)).then_inc(q_in[p], 16)
                    sp.dma_start(f32(k_rows[rows, p]),
                                 scr["k"][u, r // 2].rearrange("(i d) t -> d i t", d=D)).then_inc(k_in[p], 16)

            def load_v(b, p):
                if not known(b, 2):
                    sp.wait_ge(valued, STEPS * (b - 1))
                sp.dma_start(v_sb[:, p], scr["v"][b].rearrange("c p e -> p c e")).then_inc(v_in[p], 16)

            def load_mod(b, p):
                if not known(b, 2):
                    sp.wait_ge(summed, TC * (b - 1))
                sp.dma_start(mod[:, p], mod_scr[b].partition_broadcast(P)).then_inc(mod_in[p], 16)

            def load_x(b, c):
                if not (known(b, 1) and c < 2):
                    sp.wait_ge(rotated, TC * b + c - 1)
                sp.dma_start(x_s[:, c % 2], x[b, c * P:(c + 1) * P, :]).then_inc(x_in[c % 2], 16)

            def store(b, c):
                sp.wait_ge(rotated, TC * b + c + 1)
                sp.dma_start(out[b, c * P:(c + 1) * P, :], acc[:, c % 2]).then_inc(stored[c % 2], 16)

            def batch(b, p, first=False, last=False):
                for g in range(NG):
                    if not first:
                        load_x(b - 1, g)
                    if not (last and g >= NG - 2):
                        load_unit(NG * b + g + 2, g)
                    if g == 0 and not last:
                        load_v(b + 1, 1 - p)
                    if g == 1:
                        load_mod(b, p)
                    if g > 0 and not first:
                        store(b - 1, g - 1)
                    if g == 0 and not known(b, 2):
                        store(b - 2, TC - 1)

            load_unit(0, 0)
            load_v(0, 0)
            load_unit(1, 1)
            batch(0, 0, first=True)
            batch(1, 1)
            with sp.Fori(2, B - 3, 2) as b:
                batch(b, 0)
                batch(b + 1, 1)
            batch(B - 2, 0)
            batch(B - 1, 1, last=True)
            for c in range(TC):
                load_x(B - 1, c)
                if c == 0:
                    store(B - 2, TC - 1)
                else:
                    store(B - 1, c - 1)
            store(B - 1, TC - 1)
            for j in range(2):
                sp.wait_ge(stored[j], 16 * TC * B // 2)

        @block.tensor
        def _(pe):
            def score(b, s, r):
                n, g, half = STEPS * b + s, s // 2, s % 2
                p, i = g % 2, r // 2
                if r == 0 and half == 0:
                    seen = 32 * (NG * b + g - p) + 64
                    pe.wait_ge(q_in[p], seen)
                    pe.wait_ge(k_in[p], seen)
                if not (known(n, 1) and r < 4):
                    pe.wait_ge(masked, TILES * n + r - 3)
                c = 2 * half + r % 2
                pe.matmul(score_ps[:, r % 4, :], q_rows[:, p, i, c * P:(c + 1) * P], k_rows[:, p, i, :],
                          start=True, stop=True).then_inc(scores, 1)

            def turn(n, s, r):
                if r % 2 == 0:
                    pe.wait_ge(exped, TILES * n + r + 2)
                if not (known(n, 1) and r < 2):
                    if r < 2:
                        moved_out(pe, n - 1, TILES - 2 + r)
                    else:
                        moved_out(pe, n, r - 2)
                for j in range(2):
                    for c in range(2):
                        key = (2 * (r % 2) + j) * P
                        last = pe.transpose(prob_ps[:, r % 2, j * HALF + c * P:j * HALF + (c + 1) * P],
                                            probs[:, s % 2, r // 2 * 2 + c, key:key + P], ident[:, :])
                last.then_inc(turned, 1)

            def value(n, s, p, bv):
                g = s // 2
                if bv is not None:
                    pe.wait_ge(v_in[p], 8 * (bv - p) + 16)
                pe.wait_ge(out_act, len(BY_ACT) * (n + 1))
                pe.wait_ge(out_dve, len(BY_DVE) * (n + 1))
                pe.wait_ge(scale_out, n + 1)
                if not known(n, 1):
                    pe.wait_ge(o_scaled, n)
                for j in range(TC):
                    for i in range(HG):
                        h = HG * g + i
                        last = pe.matmul(value_ps[i * D:(i + 1) * D, :], v_sb[:, p, j, h * D:(h + 1) * D],
                                         probs_T[:, s % 2, i, j, :], start=(j == 0), stop=(j == TC - 1))
                last.then_inc(valued, 1)

            def turn_scale(n):
                pe.wait_ge(inverted, n + 1)
                if not known(n, 1):
                    pe.wait_ge(scale_out, n)
                    pe.wait_ge(o_scaled, n)
                for c in range(2):
                    last = pe.transpose(scale_ps[:, c * P:(c + 1) * P],
                                        inv_den[:, c].rearrange("p i d -> p (i d)"), ident[:, :])
                last.then_inc(scale_turned, 1)

            def project(b, p, c, k):
                if k == 0:
                    pe.wait_ge(o_ready, STEPS * b + STEPS - 1 + c // 2)
                    if not (known(b, 1) and c == 0):
                        pe.wait_ge(scaled_ready, TC * b + c)
                t = slice(c * P, (c + 1) * P)
                y = y_ps[:, :]
                pe.matmul(y, o_hi[:, p, k, t], wo_hi[:, k, :], start=(k == 0), stop=False)
                pe.matmul(y, o_hi[:, p, k, t], wo_lo[:, k, :], start=False, stop=False)
                last = pe.matmul(y, o_lo[:, p, k, t], wo_hi[:, k, :], start=False, stop=(k == KC - 1))
                if k == KC - 1:
                    last.then_inc(y_ready, 1)

            def batch(b, p, first=False, last=False):
                for s in range(STEPS):
                    n = STEPS * b + s
                    for r in range(TILES):
                        if tile_ahead(b, s, r + SCORE_AHEAD, last):
                            score(*tile_ahead(b, s, r + SCORE_AHEAD, last))
                        if r % 2 == 0 and s % 2 == 1 and not first:
                            project(b - 1, 1 - p, s // 2, r // 2)
                        if r == 2 and s > 0:
                            value(n - 1, s - 1, p, b if s == 1 else None)
                        if r == 2 and s == 0 and not first:
                            value(n - 1, STEPS - 1, 1 - p, None)
                        if r >= 1:
                            turn(n, s, r - 1)
                        if r == 6:
                            turn_scale(n)
                    turn(n, s, TILES - 1)

            for r in range(TILES + SCORE_AHEAD):
                score(0, r // TILES, r % TILES)
            batch(0, 0, first=True)
            batch(1, 1)
            with pe.Fori(2, B - 3, 2) as b:
                batch(b, 0)
                batch(b + 1, 1)
            batch(B - 2, 0)
            batch(B - 1, 1, last=True)
            value(STEPS * B - 1, STEPS - 1, 1, None)
            for c in range(TC):
                for k in range(KC):
                    project(B - 1, 1, c, k)

        @block.vector
        def _(dve):
            def mask(b, s, r):
                n = STEPS * b + s
                dve.wait_ge(scores, TILES * n + r + 1)
                if not known(n, 2):
                    dve.wait_ge(turned, TILES * (n - 2) + r // 2 * 2 + 2)
                take_waits(dve)
                c = 2 * (s % 2) + r % 2
                dve.tensor_tensor_reduce(probs[:, s % 2, r, :], score_ps[:, r % 4, :], mask_bias[:, c, :], 1.0, 3e38,
                                         ALU.add, ALU.min, least[:, s % 2, r:r + 1]).then_inc(masked, 1)

            def invert(n, s):
                dve.wait_ge(exped, TILES * (n + 1))
                if not known(n, 1):
                    dve.wait_ge(scale_turned, n)
                dve.reciprocal(inv_sum[:, :, :], den[:, s % 2].rearrange("p (i c) -> p c i", c=2)).then_inc(inv_ready, 1)
                dve.wait_ge(inv_ready, n + 1)
                dve.tensor_copy(inv_den[:, :, :, :], inv_sum[:, :, :].unsqueeze(3).to_broadcast([P, 2, HG, D])
                                ).then_inc(inverted, 1)

            def move_out(n, s, r):
                dve.wait_ge(turned, TILES * n + r + 1)
                if not known(n, 2):
                    dve.wait_ge(valued, n - 1)
                dve.tensor_copy(probs_T[:, s % 2, r // 2, 2 * (r % 2):2 * (r % 2) + 2, :],
                                prob_ps[:, r % 2, :].rearrange("p (j t) -> p j t", j=2)).then_inc(out_dve, 1)

            def scale(n, s):
                dve.wait_ge(valued, n + 1)
                dve.wait_ge(scale_out, n + 1)
                if not known(n, 2):
                    dve.wait_ge(o_ready, n - 1)
                dve.tensor_tensor(o_T[:, s % 2], value_ps, scale_T[:, :], ALU.mult).then_inc(o_scaled, 1)

            def rescale(b, p, c):
                m = TC * b + c
                if c == 0:
                    dve.wait_ge(mod_in[p], 8 * (b - p) + 16)
                dve.wait_ge(squared, m + 1)
                if not known(m, 1):
                    dve.wait_ge(summed, m)
                dve.tensor_tensor(scaled[:, :], y_ps[:, :], mod[:, p, E:], ALU.mult).then_inc(scaled_ready, 1)

            def residual(b, p, c):
                m = TC * b + c
                dve.wait_ge(scaled_ready, m + 1)
                dve.wait_ge(rstd_ready, m + 1)
                dve.wait_ge(shifted, m + 1)
                dve.scalar_tensor_tensor(x_s[:, c % 2], scaled[:, :], rstd[:, c % 2:c % 2 + 1], x_s[:, c % 2],
                                         ALU.mult, ALU.add).then_inc(summed, 1)

            def batch(b, p, first=False, last=False):
                for s in range(STEPS):
                    n = STEPS * b + s
                    for r in range(TILES):
                        if tile_ahead(b, s, r + MASK_AHEAD, last):
                            mask(*tile_ahead(b, s, r + MASK_AHEAD, last))
                        if r == 1:
                            invert(n, s)
                        if r == 4 and not (first and s == 0):
                            scale(n - 1, s - 1)
                        if r >= 1 and r - 1 in BY_DVE:
                            move_out(n, s, r - 1)
                        if r == 2 and chunk_before(b, p, s):
                            rescale(*chunk_before(b, p, s))
                        if r == 6 and chunk_before(b, p, s):
                            residual(*chunk_before(b, p, s))
                    if TILES - 1 in BY_DVE:
                        move_out(n, s, TILES - 1)

            for r in range(TILES + MASK_AHEAD):
                mask(0, r // TILES, r % TILES)
            batch(0, 0, first=True)
            batch(1, 1)
            with dve.Fori(2, B - 3, 2) as b:
                batch(b, 0)
                batch(b + 1, 1)
            batch(B - 2, 0)
            batch(B - 1, 1, last=True)
            rescale(B - 2, 0, TC - 1)
            scale(STEPS * B - 1, STEPS - 1)
            residual(B - 2, 0, TC - 1)
            for c in range(TC):
                rescale(B - 1, 1, c)
                residual(B - 1, 1, c)

        @block.scalar
        def _(act):
            def exp(n, s, r):
                act.wait_ge(masked, TILES * n + r + 1)
                if r == 0 and not known(n, 2):
                    act.wait_ge(inverted, n - 1)
                act.activation(probs[:, s % 2, r, :], probs[:, s % 2, r, :], ACT.Exp, bias=least[:, s % 2, r:r + 1],
                               scale=-1.0, accum_out=den[:, s % 2, r:r + 1]).then_inc(exped, 1)

            def move_out(n, s, r):
                act.wait_ge(turned, TILES * n + r + 1)
                if not known(n, 2):
                    act.wait_ge(valued, n - 1)
                act.activation(probs_T[:, s % 2, r // 2, 2 * (r % 2):2 * (r % 2) + 2, :],
                               prob_ps[:, r % 2, :].rearrange("p (j t) -> p j t", j=2), ACT.Copy).then_inc(out_act, 1)

            def scale_out_(n):
                act.wait_ge(scale_turned, n + 1)
                if not known(n, 1):
                    act.wait_ge(o_scaled, n)
                act.activation(scale_T[:, :], scale_ps, ACT.Copy).then_inc(scale_out, 1)

            def square(b, p, c):
                m = TC * b + c
                act.wait_ge(y_ready, m + 1)
                if not known(m, 1):
                    act.wait_ge(squared, m)
                if not known(m, 2):
                    act.wait_ge(mean_ready, m - 1)
                act.activation(junk[:, :], y_ps[:, :], ACT.Square,
                               accum_out=sum_sq[:, c % 2:c % 2 + 1]).then_inc(squared, 1)

            def batch(b, p, first=False, last=False):
                for s in range(STEPS):
                    n = STEPS * b + s
                    for r in range(TILES):
                        if not (last and s == STEPS - 1):
                            exp(n + 1, s + 1, r)
                        if r >= 1 and r - 1 in BY_ACT:
                            move_out(n, s, r - 1)
                        if r == 7:
                            scale_out_(n)
                        if r == 0 and chunk_before(b, p, s):
                            square(*chunk_before(b, p, s))
                    if TILES - 1 in BY_ACT:
                        move_out(n, s, TILES - 1)

            for r in range(TILES):
                exp(0, 0, r)
            batch(0, 0, first=True)
            batch(1, 1)
            with act.Fori(2, B - 3, 2) as b:
                batch(b, 0)
                batch(b + 1, 1)
            batch(B - 2, 0)
            batch(B - 1, 1, last=True)
            square(B - 2, 0, TC - 1)
            for c in range(TC):
                square(B - 1, 1, c)

        @block.gpsimd
        def _(pool):
            def split(b, p, s):
                n = STEPS * b + s
                g, half = s // 2, s % 2
                t = slice(half * HALF, (half + 1) * HALF)
                if s == 0 and not known(b, 2):
                    pool.wait_ge(y_ready, TC * (b - 1))
                pool.wait_ge(o_scaled, n + 1)
                take_waits(pool)
                pool.tensor_copy(o_hi[:, p, g, t], o_T[:, s % 2]).then_inc(o_hi_ready, 1)
                pool.wait_ge(o_hi_ready, n + 1)
                pool.tensor_tensor(o_lo[:, p, g, t], o_T[:, s % 2], f32(o_hi[:, p, g, t]),
                                   ALU.subtract).then_inc(o_ready, 1)

            def shift(b, p, c):
                m = TC * b + c
                if c == 0:
                    pool.wait_ge(mod_in[p], 8 * (b - p) + 16)
                pool.wait_ge(x_in[c % 2], 16 * (2 * b + c // 2 + 1))
                pool.tensor_tensor(x_s[:, c % 2], x_s[:, c % 2], mod[:, p, 0:E], ALU.add).then_inc(shifted, 1)

            def rms(b, p, c):
                m = TC * b + c
                pool.wait_ge(squared, m + 1)
                take_waits(pool)
                pool.tensor_scalar(mean_sq[:, c % 2:c % 2 + 1], sum_sq[:, c % 2:c % 2 + 1], 1.0 / E, RMS_EPS,
                                   ALU.mult, ALU.add).then_inc(mean_ready, 1)
                pool.wait_ge(mean_ready, m + 1)
                if not known(m, 2):
                    pool.wait_ge(summed, m - 1)
                pool.tensor_tensor(rstd[:, c % 2:c % 2 + 1], mean_sq[:, c % 2:c % 2 + 1], neg_half[:, :],
                                   ALU.pow).then_inc(rstd_ready, 1)

            def rotate(b, p, c):
                m = TC * b + c
                pool.wait_ge(summed, m + 1)
                if not known(m, 2):
                    pool.wait_ge(stored[c % 2], 16 * (2 * b + c // 2))
                if not known(m, 1):
                    pool.wait_ge(rotated, m)
                for j in range(4):
                    pool.tensor_tensor(mix[:, j, :].rearrange("p (i d) -> p i d", i=4), rot[:, j],
                                       x_s[:, c % 2, j * C:(j + 1) * C].unsqueeze(1).to_broadcast([P, 4, C]),
                                       ALU.mult).then_inc(mixing, 1)
                pool.wait_ge(mixing, 4 * m + 4)
                pool.tensor_tensor(mix[:, 0:2, :], mix[:, 0:2, :], mix[:, 2:4, :], ALU.add).then_inc(paired, 1)
                pool.wait_ge(paired, m + 1)
                pool.tensor_tensor(acc[:, c % 2], mix[:, 0, :], mix[:, 1, :], ALU.add).then_inc(rotated, 1)

            def batch(b, p, first=False):
                for s in range(STEPS):
                    if chunk_before(b, p, s):
                        rms(*chunk_before(b, p, s))
                    if s > 0:
                        split(b, p, s - 1)
                    elif not first:
                        split(b - 1, 1 - p, STEPS - 1)
                    if s % 2 == 0 and not first:
                        shift(b - 1, 1 - p, s // 2)
                    if s % 2 == 1 and chunk_before(b, p, s - 1):
                        rotate(*chunk_before(b, p, s - 1))

            pool.memset(neg_half[:, :], -0.5).then_inc(half_set, 1)
            pool.wait_ge(half_set, 1)
            batch(0, 0, first=True)
            batch(1, 1)
            with pool.Fori(2, B - 3, 2) as b:
                batch(b, 0)
                batch(b + 1, 1)
            batch(B - 2, 0)
            batch(B - 1, 1)
            rms(B - 2, 0, TC - 1)
            split(B - 1, 1, STEPS - 1)
            shift(B - 1, 1, 0)
            rotate(B - 2, 0, TC - 1)
            for c in range(TC):
                rms(B - 1, 1, c)
                if c + 1 < TC:
                    shift(B - 1, 1, c + 1)
                rotate(B - 1, 1, c)


def program(nc, x, xT, cond, condT, mask, wT, rms_scale, wcT, bc, q_right, gate, out):
    scr = {n: nc.dram_tensor(f"{n}_scratch", (B * NG, 2, P, S), F32, kind="Internal").ap() for n in "qk"}
    scr["v"] = nc.dram_tensor("v_scratch", (B, TC, P, E), F32, kind="Internal").ap()
    mod_scr = nc.dram_tensor("mod_scratch", (B, 2 * E), F32, kind="Internal").ap()
    with ExitStack() as ctx:
        wo_hi = ctx.enter_context(nc.sbuf_tensor("wo_hi", [P, KC, E], F32R))
        wo_lo = ctx.enter_context(nc.sbuf_tensor("wo_lo", [P, KC, E], F32R))
        mask_bias = ctx.enter_context(nc.sbuf_tensor("mask_bias", [P, TC, S], BF16))
        rot = ctx.enter_context(nc.sbuf_tensor("rot", [P, 4, 4, C], F32))
        ident = ctx.enter_context(nc.sbuf_tensor("ident", [P, P], F32))
        projections(nc, xT, wT, scr, wo_hi, wo_lo, mask, condT, cond, wcT, bc, rms_scale, q_right, gate, mod_scr,
                    mask_bias, rot, ident)
        attention(nc, x, scr, mod_scr, out, mask_bias, rot, ident, wo_hi, wo_lo)


def kernel(**inputs):
    import numpy as np
    import concourse.bacc as bacc
    from concourse.bass_utils import run_bass_kernel_spmd

    def laid(a):
        return np.ascontiguousarray(a)

    nc = bacc.Bacc("TRN2", target_bir_lowering=False, num_devices=1)
    x, cond = np.asarray(inputs["x"]), np.asarray(inputs["cond_256"])
    arrays = {
        "x": laid(x),
        "xT": laid(x.transpose(0, 2, 1)),
        "cond": laid(cond.reshape(-1)),
        "condT": laid(cond.T),
        "mask": laid(np.asarray(inputs["mask_SxS_bk1"]).view(np.int32)),
        "wqT": laid(np.asarray(inputs["L0_cond_Wq"]).T),
        "wkT": laid(np.asarray(inputs["L0_cond_Wk"]).T),
        "wvT": laid(np.asarray(inputs["L0_cond_Wv"]).T),
        "woT": laid(np.asarray(inputs["L0_cond_Wo"]).T),
        "rms_scale": laid(inputs["L0_cond_rms_scale"]),
        "wcT": laid(np.asarray(inputs["L0_cond_Wc"]).T),
        "bc": laid(inputs["L0_cond_bc"]),
        "q_right": laid(np.asarray(inputs["L1_cond_q_right"]).reshape(-1)),
        "gate": laid(np.asarray(inputs["L1_cond_spectral_gate"]).reshape(-1)),
    }
    dram = {n: nc.dram_tensor(f"in_{n}", a.shape, mybir.dt.from_np(a.dtype), kind="ExternalInput").ap()
            for n, a in arrays.items()}
    out = nc.dram_tensor("out_0", (B, S, E), F32, kind="ExternalOutput").ap()
    program(nc, dram["x"], dram["xT"], dram["cond"], dram["condT"], dram["mask"],
            [dram["wqT"], dram["wkT"], dram["wvT"], dram["woT"]], dram["rms_scale"], dram["wcT"], dram["bc"],
            dram["q_right"], dram["gate"], out)
    r = run_bass_kernel_spmd(nc, [{f"in_{n}": a for n, a in arrays.items()}], core_ids=[0])
    return r.results[0]["out_0"]
```

```python
from contextlib import ExitStack

import concourse.bass as bass
from concourse import mybir

ALU = mybir.AluOpType
ACT = mybir.ActivationFunctionType
AX_X = mybir.AxisListType.X
F32 = mybir.dt.float32
F32R = mybir.dt.float32r
BF16 = mybir.dt.bfloat16
U8 = mybir.dt.uint8

P = 128
B, S, E = 8, 512, 512
H, D = 16, 32
C = 128
KC = E // P
TC = S // P
HG = P // D
NG = H // HG
HALF = S // 2
STEPS = 2 * NG
TILES = 2 * HG
MASKED = 1e30
QSCALE = -float(D) ** -0.5
RMS_EPS, NORM_EPS = 1e-6, 1e-8


def f32(ap):
    return ap.bitcast(F32)


def projections(nc, xT, wT, scr, wo_hi, wo_lo, mask, condT, cond, wcT, bc, rms_scale, q_right, gate, mod_scr,
                mask_bias, rot, ident):
    with ExitStack() as ctx:
        def sb(name, shape, dt):
            return ctx.enter_context(nc.sbuf_tensor(name, shape, dt))

        def sem(name):
            return ctx.enter_context(nc.semaphore(name))

        w_raw = sb("w_raw", [P, 2, KC, E], F32)
        w_hi = [sb(f"w_hi_{n}", [P, KC, E], F32R) for n in "qkv"] + [wo_hi]
        w_lo = [sb(f"w_lo_{n}", [P, KC, E], F32R) for n in "qkv"] + [wo_lo]
        x_raw = sb("x_raw", [P, 2, KC, S], F32)
        x_hi = sb("x_hi", [P, 2, KC, S], F32R)
        x_lo = sb("x_lo", [P, 2, KC, S], F32R)
        qk_hi = sb("qk_hi", [P, 4, S], F32R)
        qk_lo = sb("qk_lo", [P, 4, S], F32R)
        v_out = sb("v_out", [P, 4, E], F32)
        proj = ctx.enter_context(nc.psum_tensor("proj", [P, 4, 512], F32))

        mask_words = sb("mask_words", [P, TC, S // 4], mybir.dt.int32)
        mask_u8 = mask_words[:, :, :].bitcast(U8)
        row_least = sb("row_least", [P, TC], F32)
        row_open = sb("row_open", [P, TC], F32)
        row_nan = sb("row_nan", [P, TC], F32)
        nan_part = sb("nan_part", [P, 1], F32)
        ones8 = sb("ones8", [P, B], F32)
        nan_all = sb("nan_all", [B, 1], F32)
        cT = sb("cT", [P, B], F32)
        c_sig = sb("c_sig", [P, B], F32)
        c_silu = sb("c_silu", [P, B], F32)
        wc = sb("wc", [P, 2 * E], F32)
        bc8 = sb("bc8", [B, 2 * E], F32)
        rms8 = sb("rms8", [B, E], F32)
        mod = sb("mod", [B, 2 * E], F32)
        quat = sb("quat", [P, 12, C], F32)
        square = sb("square", [P, 12, C], F32)
        neg_half = sb("neg_half", [P, 2, C], F32)
        gate_b = sb("gate_b", [P, C], F32)
        term = sb("term", [P, 4, 4, C], F32)
        left = w_raw[:, 0].rearrange("p k (i d) -> p k i d", i=4)
        right = w_raw[:, 1].rearrange("p k (j d) -> p k j d", j=4)
        mod_ps = ctx.enter_context(nc.psum_tensor("mod_ps", [P, 3, 512], F32))

        loaded = sem("loaded")
        pool_step, dve_step = sem("pool_step"), sem("dve_step")
        sig_exp, silu_ready = sem("sig_exp"), sem("silu_ready")
        nan_ready = sem("nan_ready")
        mod_matmul = sem("mod_matmul")
        mod_ready, mod_stored = sem("mod_ready"), sem("mod_stored")

        w_in = [sem(f"w_in{i}") for i in range(2)]
        x_in = [sem(f"x_in{i}") for i in range(2)]
        w_hi_ready, w_lo_ready = sem("w_hi_ready"), sem("w_lo_ready")
        x_hi_ready, x_lo_ready = sem("x_hi_ready"), sem("x_lo_ready")
        projected = sem("projected")
        v_copied = sem("v_copied")
        qk_hi_ready, qk_lo_ready = sem("qk_hi_ready"), sem("qk_lo_ready")
        v_stored = [sem(f"v_stored{i}") for i in range(4)]
        qk_stored = [sem(f"qk_stored{i}") for i in range(4)]

        VT, QKT = TC, 2 * NG
        TASKS = VT + QKT
        W_ORDER = (2, 0, 1, 3)
        LOADED = 16 * 8

        block = ctx.enter_context(nc.Block())

        @block.sync
        def _(sp):
            def load_x(b, p):
                sp.dma_start(x_raw[:, p], xT[b].rearrange("(k p) t -> p k t", p=P)).then_inc(x_in[p], 16)

            def load_w(n):
                sp.dma_start(w_raw[:, n % 2], wT[W_ORDER[n]].rearrange("(k p) e -> p k e", p=P)).then_inc(w_in[n % 2], 16)

            load_w(0)
            load_x(0, 0)
            load_w(1)
            sp.dma_start(mask_words[:, :, :], mask.rearrange("(c p) t -> p c t", p=P)).then_inc(loaded, 16)
            sp.dma_start(cT[:, :], condT).then_inc(loaded, 16)
            sp.dma_start(quat[:, 0:8, :], cond.partition_broadcast(P)).then_inc(loaded, 16)
            sp.dma_start(quat[:, 8:12, :], q_right.partition_broadcast(P)).then_inc(loaded, 16)
            sp.dma_start(gate_b[:, :], gate.partition_broadcast(P)).then_inc(loaded, 16)
            sp.dma_start(wc[:, :], wcT).then_inc(loaded, 16)
            sp.dma_start(bc8[:, :], bc.partition_broadcast(B)).then_inc(loaded, 16)
            sp.dma_start(rms8[:, :], rms_scale.partition_broadcast(B)).then_inc(loaded, 16)
            load_x(1, 1)
            for n in (2, 3):
                sp.wait_ge(w_lo_ready, n - 1)
                load_w(n)

            def store_v(b, c):
                sp.wait_ge(v_copied, VT * b + c + 1)
                sp.dma_start(scr["v"][b, c], v_out[:, c, :]).then_inc(v_stored[c], 16)

            def store_qk(b, which, g):
                j = g
                sp.wait_ge(qk_lo_ready, QKT * b + NG * which + g + 1)
                to = scr["qk"[which]][b * NG + g]
                sp.dma_start(to[0], f32(qk_hi[:, j, :])).then_inc(qk_stored[j], 16)
                sp.dma_start(to[1], f32(qk_lo[:, j, :])).then_inc(qk_stored[j], 16)

            def batch(b, p, more):
                for c in range(TC):
                    store_v(b, c)
                if more:
                    sp.wait_ge(x_lo_ready, b + 1)
                    load_x(b + 2, p)
                for which in range(2):
                    for g in range(NG):
                        store_qk(b, which, g)

            with sp.Fori(0, B - 3, 2) as b:
                batch(b, 0, True)
                batch(b + 1, 1, True)
            batch(B - 2, 0, False)
            batch(B - 1, 1, False)
            sp.wait_ge(mod_ready, 1)
            sp.dma_start(mod_scr, mod[:, :]).then_inc(mod_stored, 16)
            sp.wait_ge(mod_stored, 16)
            for j in range(4):
                sp.wait_ge(v_stored[j], 16 * B)
                sp.wait_ge(qk_stored[j], 16 * 4 * B)

        @block.scalar
        def _(act):
            def split_w(n):
                act.wait_ge(w_in[n % 2], 16 * (n // 2 + 1))
                act.activation(w_hi[W_ORDER[n]][:, :, :], w_raw[:, n % 2], ACT.Copy).then_inc(w_hi_ready, 1)

            def split_x(b, p):
                act.wait_ge(x_in[p], 8 * (b - p) + 16)
                if not (isinstance(b, int) and b < 2):
                    act.wait_ge(projected, TASKS * (b - 1))
                act.activation(x_hi[:, p], x_raw[:, p], ACT.Copy).then_inc(x_hi_ready, 1)

            def batch(b, p, more, first=False):
                for c in range(VT):
                    act.wait_ge(projected, TASKS * b + c + 1)
                    if not first:
                        act.wait_ge(v_stored[c], 16 * b)
                    act.activation(v_out[:, c, :], proj[:, c, :], ACT.Copy).then_inc(v_copied, 1)
                for m in range(QKT):
                    act.wait_ge(projected, TASKS * b + VT + m + 1)
                    if not (first and m < 4):
                        act.wait_ge(qk_stored[m % 4], 64 * b + 32 * (m // 4))
                    act.activation(qk_hi[:, m % 4, :], proj[:, m % 4, :], ACT.Copy,
                                   scale=QSCALE if m < NG else 1.0).then_inc(qk_hi_ready, 1)
                    if m == 1 and more:
                        split_x(b + 1, 1 - p)

            split_w(0)
            split_x(0, 0)
            for n in (1, 2, 3):
                split_w(n)
            act.wait_ge(loaded, LOADED)
            act.activation(c_sig[:, :], cT[:, :], ACT.Exp, scale=-1.0).then_inc(sig_exp, 1)
            batch(0, 0, True, first=True)
            with act.Fori(1, B - 2, 2) as b:
                batch(b, 1, True)
                batch(b + 1, 0, True)
            batch(B - 1, 1, False)

        @block.vector
        def _(dve):
            def split_w(n):
                dve.wait_ge(w_hi_ready, n + 1)
                dve.tensor_tensor(w_lo[W_ORDER[n]][:, :, :], w_raw[:, n % 2], f32(w_hi[W_ORDER[n]][:, :, :]),
                                  ALU.subtract).then_inc(w_lo_ready, 1)

            def split_x(b, p):
                dve.wait_ge(x_hi_ready, b + 1)
                dve.tensor_tensor(x_lo[:, p], x_raw[:, p], f32(x_hi[:, p]), ALU.subtract).then_inc(x_lo_ready, 1)

            def batch(b, p, more):
                for m in range(QKT):
                    dve.wait_ge(qk_hi_ready, QKT * b + m + 1)
                    dve.scalar_tensor_tensor(qk_lo[:, m % 4, :], proj[:, m % 4, :], QSCALE if m < NG else 1.0,
                                             f32(qk_hi[:, m % 4, :]), ALU.mult, ALU.subtract).then_inc(qk_lo_ready, 1)
                    if m == 1 and more:
                        split_x(b + 1, 1 - p)

            split_w(0)
            split_x(0, 0)
            for n in (1, 2, 3):
                split_w(n)

            done = [0]

            def link(ins):
                done[0] += 1
                ins.then_inc(dve_step, 1)
                dve.wait_ge(dve_step, done[0])

            dve.wait_ge(loaded, LOADED)
            link(dve.tensor_scalar(mask_bias[:, :, :], mask_u8, MASKED, None, ALU.mult))
            link(dve.tensor_reduce(row_least[:, :], mask_bias[:, :, :], AX_X, ALU.min))
            link(dve.tensor_scalar(row_open[:, :], row_least[:, :], MASKED / 2, None, ALU.is_lt))
            link(dve.reciprocal(row_nan[:, :], row_open[:, :]))
            link(dve.tensor_scalar(row_nan[:, :], row_nan[:, :], 0.0, None, ALU.mult))
            dve.tensor_reduce(nan_part[:, :], row_nan[:, :], AX_X, ALU.add).then_inc(nan_ready, 1)
            dve.wait_ge(sig_exp, 1)
            link(dve.tensor_scalar(c_sig[:, :], c_sig[:, :], 1.0, None, ALU.add))
            link(dve.reciprocal(c_sig[:, :], c_sig[:, :]))
            dve.tensor_tensor(c_silu[:, :], cT[:, :], c_sig[:, :], ALU.mult).then_inc(silu_ready, 1)

            with dve.Fori(0, B - 3, 2) as b:
                batch(b, 0, True)
                batch(b + 1, 1, True)
            dve.wait_ge(mod_matmul, 3)
            link(dve.tensor_copy(nan_all[:, :], mod_ps[0:B, 2, 0:1]))
            link(dve.scalar_tensor_tensor(mod[:, 0:E], mod_ps[0:B, 0, :], nan_all[:, 0:1], bc8[:, 0:E],
                                          ALU.add, ALU.add))
            link(dve.tensor_tensor(mod[:, E:], mod_ps[0:B, 1, :], bc8[:, E:], ALU.add))
            dve.scalar_tensor_tensor(mod[:, E:], mod[:, E:], 1.0, rms8[:, :], ALU.add, ALU.mult).then_inc(mod_ready, 1)
            batch(B - 2, 0, True)
            batch(B - 1, 1, False)

        @block.tensor
        def _(pe):
            def passes(out, hi, lo, other_hi, other_lo):
                for k in range(KC):
                    pe.matmul(out, hi(k), other_hi(k), start=(k == 0), stop=False)
                    pe.matmul(out, hi(k), other_lo(k), start=False, stop=False)
                    last = pe.matmul(out, lo(k), other_hi(k), start=False, stop=(k == KC - 1))
                last.then_inc(projected, 1)

            def batch(b, p, first=False):
                for c in range(VT):
                    if c == 0:
                        pe.wait_ge(x_lo_ready, b + 1)
                    if first:
                        pe.wait_ge(w_lo_ready, 1)
                    else:
                        pe.wait_ge(qk_lo_ready, QKT * b - 4 + c + 1)
                    t = slice(c * P, (c + 1) * P)
                    passes(proj[:, c, :], lambda k: x_hi[:, p, k, t], lambda k: x_lo[:, p, k, t],
                           lambda k: w_hi[2][:, k, :], lambda k: w_lo[2][:, k, :])
                for m in range(QKT):
                    if m < 4:
                        pe.wait_ge(v_copied, VT * b + m + 1)
                    else:
                        pe.wait_ge(qk_lo_ready, QKT * b + m - 3)
                    w = m // NG
                    if first and m % NG == 0:
                        pe.wait_ge(w_lo_ready, 2 + w)
                    e = slice((m % NG) * P, (m % NG + 1) * P)
                    passes(proj[:, m % 4, :], lambda k: w_hi[w][:, k, e], lambda k: w_lo[w][:, k, e],
                           lambda k: x_hi[:, p, k, :], lambda k: x_lo[:, p, k, :])

            batch(0, 0, first=True)
            pe.wait_ge(silu_ready, 1)
            pe.wait_ge(nan_ready, 2)
            for h in range(2):
                pe.matmul(mod_ps[0:B, h, :], c_silu[:, :], wc[:, h * E:(h + 1) * E],
                          start=True, stop=True).then_inc(mod_matmul, 1)
            pe.matmul(mod_ps[0:B, 2, 0:1], ones8[:, :], nan_part[:, :], start=True, stop=True).then_inc(mod_matmul, 1)
            with pe.Fori(1, B - 2, 2) as b:
                batch(b, 1)
                batch(b + 1, 0)
            batch(B - 1, 1)

        @block.gpsimd
        def _(pool):
            done = [0]

            def link(ins):
                done[0] += 1
                ins.then_inc(pool_step, 1)
                pool.wait_ge(pool_step, done[0])

            pool.memset(ones8[:, :], 1.0).then_inc(nan_ready, 1)
            pool.memset(neg_half[:, :, :], -0.5)
            link(pool.memset(ident[:, :], 0.0))
            link(pool.affine_select(out=ident[:, :], in_=ident[:, :], compare_op=ALU.not_equal, fill=1.0,
                                    base=0, pattern=[[-1, P]], channel_multiplier=1))
            pool.wait_ge(loaded, LOADED)
            link(pool.tensor_tensor(square[:, :, :], quat[:, :, :], quat[:, :, :], ALU.mult))
            link(pool.tensor_tensor(square[:, 0:4, :], square[:, 0:4, :], square[:, 4:8, :], ALU.add))
            pool.tensor_tensor(square[:, 4:6, :], square[:, 0:2, :], square[:, 2:4, :], ALU.add)
            link(pool.tensor_tensor(square[:, 6:8, :], square[:, 8:10, :], square[:, 10:12, :], ALU.add))
            sums = square[:, 4:8, :].rearrange("p (q h) d -> p q h d", h=2)
            link(pool.tensor_tensor(square[:, 0:2, :], sums[:, :, 0, :], sums[:, :, 1, :], ALU.add))
            link(pool.tensor_scalar(square[:, 0:2, :], square[:, 0:2, :], 1.0, NORM_EPS, ALU.mult, ALU.add))
            link(pool.tensor_tensor(square[:, 2:4, :], square[:, 0:2, :], neg_half[:, :, :], ALU.pow))
            pool.tensor_tensor(quat[:, 0:4, :], quat[:, 0:4, :],
                               square[:, 2, :].unsqueeze(1).to_broadcast([P, 4, C]), ALU.mult)
            link(pool.tensor_tensor(square[:, 8, :], square[:, 3, :], gate_b[:, :], ALU.mult))
            link(pool.tensor_tensor(quat[:, 8:12, :], quat[:, 8:12, :],
                                    square[:, 8, :].unsqueeze(1).to_broadcast([P, 4, C]), ALU.mult))
            by_left = [[(0, 1), (1, -1), (2, -1), (3, -1)], [(1, 1), (0, 1), (3, -1), (2, 1)],
                       [(2, 1), (3, 1), (0, 1), (1, -1)], [(3, 1), (2, -1), (1, 1), (0, 1)]]
            by_right = [[(0, 1), (1, 1), (2, 1), (3, 1)], [(1, -1), (0, 1), (3, -1), (2, 1)],
                        [(2, -1), (3, 1), (0, 1), (1, -1)], [(3, -1), (2, -1), (1, 1), (0, 1)]]
            pool.wait_ge(w_lo_ready, 4)
            for i in range(4):
                for k in range(4):
                    q, sign = by_left[i][k]
                    pool.tensor_scalar(left[:, k, i, :], quat[:, q, :], float(sign), 0.0, ALU.mult, ALU.add)
            for k in range(4):
                for j in range(4):
                    q, sign = by_right[k][j]
                    last = pool.tensor_scalar(right[:, k, j, :], quat[:, 8 + q, :], float(sign), 0.0, ALU.mult, ALU.add)
            link(last)

            for k in range(4):
                to = rot if k == 0 else term
                for j in range(4):
                    last = pool.tensor_tensor(to[:, j], left[:, k], right[:, k, j, :].unsqueeze(1).to_broadcast([P, 4, C]),
                                              ALU.mult)
                link(last)
                if k > 0:
                    link(pool.tensor_tensor(rot[:, :, :, :], rot[:, :, :, :], term[:, :, :, :], ALU.add))
            for i in range(4):
                link(pool.tensor_scalar(rot[:, i, i, :], rot[:, i, i, :], 1.0, 1.0, ALU.mult, ALU.add))


def attention(nc, x, scr, mod_scr, out, mask_bias, rot, ident, wo_hi, wo_lo):
    with ExitStack() as ctx:
        def sb(name, shape, dt=F32):
            return ctx.enter_context(nc.sbuf_tensor(name, shape, dt))

        def ps(name, shape):
            return ctx.enter_context(nc.psum_tensor(name, shape, F32))

        def sem(name):
            return ctx.enter_context(nc.semaphore(name))

        q_rows = sb("q_rows", [P, 2, HG, S], F32R)
        k_rows = sb("k_rows", [P, 2, HG, S], F32R)
        v_sb = sb("v_sb", [P, 2, TC, E], F32)
        probs = sb("probs", [P, 2, TILES, S])
        den = sb("den", [P, 2, TILES])
        least = sb("least", [P, 2, TILES])
        inv_sum = sb("inv_sum", [P, 2, HG])
        inv_den = sb("inv_den", [P, 2, HG, D])
        probs_T = sb("probs_T", [P, 2, HG, TC, HALF])
        raw_T = sb("raw_T", [P, 2, 2, HALF])
        o_T = sb("o_T", [P, 2, HALF])
        o_hi = sb("o_hi", [P, 2, NG, S], F32R)
        o_lo = sb("o_lo", [P, 2, NG, S], F32R)
        mod = sb("mod_b", [P, 2, 2 * E])
        x_s = sb("x_s", [P, 2, E])
        scaled = sb("scaled", [P, E])
        junk = sb("junk", [P, E], BF16)
        sum_sq = sb("sum_sq", [P, 2])
        mean_sq = sb("mean_sq", [P, 2])
        rstd = sb("rstd", [P, 2])
        tail_sum_sq = sb("tail_sum_sq", [P, TC])
        tail_mean_sq = sb("tail_mean_sq", [P, TC])
        tail_inv_rms = sb("tail_inv_rms", [P, TC])
        neg_half = sb("neg_half2", [P, 1])
        mix = sb("mix", [P, 4, E])
        acc = sb("acc", [P, 2, E])

        score_ps = ps("score_ps", [P, 4, 512])
        prob_ps = ps("prob_ps", [P, 2, 512])
        out_ps = ps("out_ps", [P, 2, HALF])
        value_ps, scale_ps = out_ps[:, 0, :], out_ps[:, 1, :]
        y_ps = ps("y_ps", [P, 512])

        q_in = [sem(f"q_in{i}") for i in range(2)]
        k_in = [sem(f"k_in{i}") for i in range(2)]
        v_in = [sem(f"v_in{i}") for i in range(2)]
        mod_in = [sem(f"mod_in{i}") for i in range(2)]
        x_in = [sem(f"xc_in{i}") for i in range(2)]
        stored = [sem(f"stored{i}") for i in range(2)]
        scores = sem("scores")
        masked = sem("masked")
        exped = sem("exped")
        inv_ready = sem("inv_ready2")
        inverted = sem("inverted")
        turned = sem("turned")
        out_act, out_dve = sem("out_act"), sem("out_dve")
        scale_turned = sem("scale_turned")
        valued = sem("valued")
        raw_out = sem("raw_out")
        o_scaled = sem("o_scaled")
        o_hi_ready, o_ready = sem("o_hi_ready"), sem("o_ready")
        y_ready = sem("y_ready")
        squared = sem("squared")
        mean_ready, rstd_ready = sem("mean_ready"), sem("rstd_ready")
        scaled_ready = sem("scaled_ready")
        shifted = sem("shifted")
        summed = sem("summed")
        half_set = sem("half_set")
        passed = sem("passed")
        mixing = sem("mixing")
        paired = sem("paired")
        rotated = sem("rotated")

        SCORE_AHEAD, MASK_AHEAD = 3, 2
        PROJECT_AT, VALUE_AT = (0, 1), (2, 3, 4, 5)
        TURN_SCALE_AT, INVERT_AT = 6, 7
        VALUES_OUT_AT, SQUARE_AT, RESCALE_AT, RESIDUAL_AT = 6, 3, 5, 2
        BY_ACT = ((1, 3, 5, 7), (0, 2, 4, 6, 7))
        BY_DVE = tuple(tuple(r for r in range(TILES) if r not in mine) for mine in BY_ACT)

        def count_out(by, b, s, among):
            return (len(by[0]) + len(by[1])) * (NG * b + s // 2) + (s % 2) * len(by[0]) + among

        def moved_out(eng, b, s, r):
            if r in BY_ACT[s % 2]:
                eng.wait_ge(out_act, count_out(BY_ACT, b, s, BY_ACT[s % 2].index(r) + 1))
            else:
                eng.wait_ge(out_dve, count_out(BY_DVE, b, s, BY_DVE[s % 2].index(r) + 1))

        def take_waits(eng):
            eng.sem_inc(passed, 1)

        def known(v, least_value):
            return isinstance(v, int) and v < least_value

        def rotation_products(eng, to, chunk):
            return eng.tensor_tensor(to.rearrange("p j (i d) -> p j i d", i=4), rot[:, :, :, :],
                                     chunk.rearrange("p (j d) -> p j d", j=4).unsqueeze(2).to_broadcast([P, 4, 4, C]),
                                     ALU.mult)

        def tile_ahead(b, s, r, last):
            s, r = s + 1 + r // TILES, r % TILES
            if s < STEPS:
                return b, s, r
            return None if last else (b + 1, s - STEPS, r)

        def chunk_before(b, p, s):
            if s % 2 or known(b, 1) or (s == 0 and known(b, 2)):
                return None
            return (b - 1, 1 - p, s // 2 - 1) if s else (b - 2, p, TC - 1)

        tail_scaled = [probs[:, 0, c, :] for c in range(TC)]
        tail_x = [probs[:, 0, TC + c, :] for c in range(TC)]
        tail_out = [probs[:, 1, TC + c, :] for c in range(TC)]
        tail_mix = probs[:, 1, 0:TC, :]
        tail_in = [sem(f"tail_in{c}") for c in range(TC)]
        tail_stored = [sem(f"tail_stored{c}") for c in range(TC)]
        tail_squared, tail_scaled_ready = sem("tail_squared"), sem("tail_scaled_ready")
        tail_mean, tail_rstd = sem("tail_mean"), sem("tail_rstd")
        tail_shifted, tail_summed = sem("tail_shifted"), sem("tail_summed")
        tail_mixed, tail_paired = sem("tail_mixed"), sem("tail_paired")
        dve_rotated = sem("dve_rotated")
        BY_POOL = 1
        ROTATED = {0: 2, 2: 3, 3: 4}
        ALL_TURNED = TILES * STEPS * B

        block = ctx.enter_context(nc.Block())

        @block.sync
        def _(sp):
            def load_unit(u, g):
                p = g % 2
                if not known(u, 2):
                    sp.wait_ge(scores, TILES * 2 * (u - 1))
                for r in range(4):
                    rows = slice(r * D, (r + 1) * D)
                    sp.dma_start(f32(q_rows[rows, p]),
                                 scr["q"][u, r % 2].rearrange("(i d) t -> d i t", d=D)).then_inc(q_in[p], 16)
                    sp.dma_start(f32(k_rows[rows, p]),
                                 scr["k"][u, r // 2].rearrange("(i d) t -> d i t", d=D)).then_inc(k_in[p], 16)

            def load_v(b, p):
                if not known(b, 2):
                    sp.wait_ge(valued, STEPS * (b - 1))
                sp.dma_start(v_sb[:, p], scr["v"][b].rearrange("c p e -> p c e")).then_inc(v_in[p], 16)

            def load_mod(b, p):
                if not known(b, 2):
                    sp.wait_ge(summed, TC * (b - 1))
                sp.dma_start(mod[:, p], mod_scr[b].partition_broadcast(P)).then_inc(mod_in[p], 16)

            def load_x(b, c):
                if not (known(b, 1) and c < 2):
                    sp.wait_ge(rotated, TC * b + c - 1)
                sp.dma_start(x_s[:, c % 2], x[b, c * P:(c + 1) * P, :]).then_inc(x_in[c % 2], 16)

            def store(b, c):
                sp.wait_ge(rotated, TC * b + c + 1)
                sp.dma_start(out[b, c * P:(c + 1) * P, :], acc[:, c % 2]).then_inc(stored[c % 2], 16)

            def batch(b, p, first=False, last=False):
                for g in range(NG):
                    if not first:
                        load_x(b - 1, g)
                    if not (last and g >= NG - 2):
                        load_unit(NG * b + g + 2, g)
                    if g == 0 and not last:
                        load_v(b + 1, 1 - p)
                    if g == 1:
                        load_mod(b, p)
                    if g > 0 and not first:
                        store(b - 1, g - 1)
                    if g == 0 and not known(b, 2):
                        store(b - 2, TC - 1)

            load_unit(0, 0)
            load_v(0, 0)
            load_unit(1, 1)
            batch(0, 0, first=True)
            batch(1, 1)
            with sp.Fori(2, B - 3, 2) as b:
                batch(b, 0)
                batch(b + 1, 1)
            batch(B - 2, 0)
            batch(B - 1, 1, last=True)
            sp.wait_ge(turned, ALL_TURNED - TILES)
            for c in range(TC):
                sp.dma_start(tail_x[c], x[B - 1, c * P:(c + 1) * P, :]).then_inc(tail_in[c], 16)
            sp.wait_ge(dve_rotated, 1)
            sp.dma_start(out[B - 2, (TC - 1) * P:TC * P, :], acc[:, 1]).then_inc(stored[1], 16)
            for c in (0, 2, BY_POOL, 3):
                if c == BY_POOL:
                    sp.wait_ge(rotated, TC * (B - 1))
                else:
                    sp.wait_ge(dve_rotated, ROTATED[c])
                sp.dma_start(out[B - 1, c * P:(c + 1) * P, :], tail_out[c]).then_inc(tail_stored[c], 16)
            for j in range(2):
                sp.wait_ge(stored[j], 16 * TC * (B - 1) // 2)
            for c in range(TC):
                sp.wait_ge(tail_stored[c], 16)

        @block.tensor
        def _(pe):
            def score(b, s, r):
                n, g, half = STEPS * b + s, s // 2, s % 2
                p, i = g % 2, r // 2
                if r == 0 and half == 0:
                    seen = 32 * (NG * b + g - p) + 64
                    pe.wait_ge(q_in[p], seen)
                    pe.wait_ge(k_in[p], seen)
                if not (known(n, 1) and r < 4):
                    pe.wait_ge(masked, TILES * n + r - 3)
                c = 2 * half + r % 2
                pe.matmul(score_ps[:, r % 4, :], q_rows[:, p, i, c * P:(c + 1) * P], k_rows[:, p, i, :],
                          start=True, stop=True).then_inc(scores, 1)

            def turn(b, s, r):
                n = STEPS * b + s
                if r % 2 == 0:
                    pe.wait_ge(exped, TILES * n + r + 2)
                if not (known(n, 1) and r < 2):
                    if r < 2:
                        moved_out(pe, b, s - 1, TILES - 2 + r)
                    else:
                        moved_out(pe, b, s, r - 2)
                for j in range(2):
                    for c in range(2):
                        key = (2 * (r % 2) + j) * P
                        last = pe.transpose(prob_ps[:, r % 2, j * HALF + c * P:j * HALF + (c + 1) * P],
                                            probs[:, s % 2, r // 2 * 2 + c, key:key + P], ident[:, :])
                last.then_inc(turned, 1)

            def value(b, s, p, j):
                n, g = STEPS * b + s, s // 2
                if s == 0 and j == 0:
                    pe.wait_ge(v_in[p], 8 * (b - p) + 16)
                if j == 0:
                    pe.wait_ge(out_act, count_out(BY_ACT, b, s, len(BY_ACT[s % 2])))
                    pe.wait_ge(out_dve, count_out(BY_DVE, b, s, len(BY_DVE[s % 2])))
                    if not known(n, 1):
                        pe.wait_ge(raw_out, n)
                for i in range(HG):
                    h = HG * g + i
                    last = pe.matmul(value_ps[i * D:(i + 1) * D, :], v_sb[:, p, j, h * D:(h + 1) * D],
                                     probs_T[:, s % 2, i, j, :], start=(j == 0), stop=(j == TC - 1))
                if j == TC - 1:
                    last.then_inc(valued, 1)

            def turn_scale(n):
                pe.wait_ge(inverted, n + 1)
                if not known(n, 1):
                    pe.wait_ge(raw_out, n)
                for c in range(2):
                    last = pe.transpose(scale_ps[:, c * P:(c + 1) * P],
                                        inv_den[:, c].rearrange("p i d -> p (i d)"), ident[:, :])
                last.then_inc(scale_turned, 1)

            def project(b, p, c, k, y):
                if k == 0:
                    pe.wait_ge(o_ready, STEPS * b + STEPS - 1 + c // 2)
                    if y is y_ps and not (known(b, 1) and c == 0):
                        pe.wait_ge(scaled_ready, TC * b + c)
                t = slice(c * P, (c + 1) * P)
                pe.matmul(y[:, :], o_hi[:, p, k, t], wo_hi[:, k, :], start=(k == 0), stop=False)
                pe.matmul(y[:, :], o_hi[:, p, k, t], wo_lo[:, k, :], start=False, stop=False)
                last = pe.matmul(y[:, :], o_lo[:, p, k, t], wo_hi[:, k, :], start=False, stop=(k == KC - 1))
                if k == KC - 1:
                    last.then_inc(y_ready, 1)

            def batch(b, p, first=False, last=False):
                for s in range(STEPS):
                    n = STEPS * b + s
                    for r in range(TILES):
                        if tile_ahead(b, s, r + SCORE_AHEAD, last):
                            score(*tile_ahead(b, s, r + SCORE_AHEAD, last))
                        if r in PROJECT_AT and s % 2 == 1 and not first:
                            project(b - 1, 1 - p, s // 2, PROJECT_AT.index(r), y_ps)
                        if r in PROJECT_AT and chunk_before(b, p, s):
                            project(*chunk_before(b, p, s), 2 + PROJECT_AT.index(r), y_ps)
                        if r in VALUE_AT and s > 0:
                            value(b, s - 1, p, VALUE_AT.index(r))
                        if r in VALUE_AT and s == 0 and not first:
                            value(b - 1, STEPS - 1, 1 - p, VALUE_AT.index(r))
                        if r >= 1:
                            turn(b, s, r - 1)
                        if r == TURN_SCALE_AT and not (first and s == 0):
                            turn_scale(n - 1)
                    turn(b, s, TILES - 1)

            for r in range(TILES + SCORE_AHEAD):
                score(0, r // TILES, r % TILES)
            batch(0, 0, first=True)
            batch(1, 1)
            with pe.Fori(2, B - 3, 2) as b:
                batch(b, 0)
                batch(b + 1, 1)
            batch(B - 2, 0)
            batch(B - 1, 1, last=True)
            for k in (2, 3):
                project(B - 2, 0, TC - 1, k, y_ps)
            for j in range(TC):
                value(B - 1, STEPS - 1, 1, j)
            turn_scale(STEPS * B - 1)
            pe.wait_ge(masked, TILES * STEPS * B)
            for c in range(TC):
                for k in range(KC):
                    project(B - 1, 1, c, k, score_ps[:, c, :])

        @block.vector
        def _(dve):
            def mask(b, s, r):
                n = STEPS * b + s
                dve.wait_ge(scores, TILES * n + r + 1)
                if not known(n, 2):
                    dve.wait_ge(turned, TILES * (n - 2) + r // 2 * 2 + 2)
                take_waits(dve)
                c = 2 * (s % 2) + r % 2
                dve.tensor_tensor_reduce(probs[:, s % 2, r, :], score_ps[:, r % 4, :], mask_bias[:, c, :], 1.0, 3e38,
                                         ALU.add, ALU.min, least[:, s % 2, r:r + 1]).then_inc(masked, 1)

            def invert(n, s):
                dve.wait_ge(exped, TILES * (n + 1))
                if not known(n, 1):
                    dve.wait_ge(scale_turned, n)
                dve.reciprocal(inv_sum[:, :, :], den[:, s % 2].rearrange("p (i c) -> p c i", c=2)).then_inc(inv_ready, 1)
                dve.wait_ge(inv_ready, n + 1)
                dve.tensor_copy(inv_den[:, :, :, :], inv_sum[:, :, :].unsqueeze(3).to_broadcast([P, 2, HG, D])
                                ).then_inc(inverted, 1)

            def move_out(n, s, r):
                dve.wait_ge(turned, TILES * n + r + 1)
                if not known(n, 2):
                    dve.wait_ge(valued, n - 1)
                dve.tensor_copy(probs_T[:, s % 2, r // 2, 2 * (r % 2):2 * (r % 2) + 2, :],
                                prob_ps[:, r % 2, :].rearrange("p (j t) -> p j t", j=2)).then_inc(out_dve, 1)

            def rescale(b, p, c):
                m = TC * b + c
                if c == 0:
                    dve.wait_ge(mod_in[p], 8 * (b - p) + 16)
                dve.wait_ge(squared, m + 1)
                if not known(m, 1):
                    dve.wait_ge(summed, m)
                dve.tensor_tensor(scaled[:, :], y_ps[:, :], mod[:, p, E:], ALU.mult).then_inc(scaled_ready, 1)

            def residual(b, p, c):
                m = TC * b + c
                dve.wait_ge(scaled_ready, m + 1)
                dve.wait_ge(rstd_ready, m + 1)
                dve.wait_ge(shifted, m + 1)
                dve.scalar_tensor_tensor(x_s[:, c % 2], scaled[:, :], rstd[:, c % 2:c % 2 + 1], x_s[:, c % 2],
                                         ALU.mult, ALU.add).then_inc(summed, 1)

            def batch(b, p, first=False, last=False):
                for s in range(STEPS):
                    n = STEPS * b + s
                    for r in range(TILES):
                        if tile_ahead(b, s, r + MASK_AHEAD, last):
                            mask(*tile_ahead(b, s, r + MASK_AHEAD, last))
                        if r == INVERT_AT:
                            invert(n, s)
                        if r >= 1 and r - 1 in BY_DVE[s % 2]:
                            move_out(n, s, r - 1)
                        if r == RESCALE_AT and chunk_before(b, p, s):
                            rescale(*chunk_before(b, p, s))
                        if r == RESIDUAL_AT and s % 2 == 1 and chunk_before(b, p, s - 1):
                            residual(*chunk_before(b, p, s - 1))
                    if TILES - 1 in BY_DVE[s % 2]:
                        move_out(n, s, TILES - 1)

            for r in range(TILES + MASK_AHEAD):
                mask(0, r // TILES, r % TILES)
            batch(0, 0, first=True)
            batch(1, 1)
            with dve.Fori(2, B - 3, 2) as b:
                batch(b, 0)
                batch(b + 1, 1)
            batch(B - 2, 0)
            batch(B - 1, 1, last=True)
            rescale(B - 2, 0, TC - 1)
            residual(B - 2, 0, TC - 1)

            def rotate(i, chunk, to):
                dve.wait_ge(turned, ALL_TURNED)
                if i > 0:
                    dve.wait_ge(dve_rotated, i)
                rotation_products(dve, tail_mix, chunk).then_inc(tail_mixed, 1)
                dve.wait_ge(tail_mixed, i + 1)
                dve.tensor_tensor(tail_mix[:, 0:2, :], tail_mix[:, 0:2, :], tail_mix[:, 2:4, :],
                                  ALU.add).then_inc(tail_paired, 1)
                dve.wait_ge(tail_paired, i + 1)
                dve.tensor_tensor(to, tail_mix[:, 0, :], tail_mix[:, 1, :], ALU.add).then_inc(dve_rotated, 1)

            def tail_rescale(c):
                dve.wait_ge(tail_squared, c + 1)
                dve.tensor_tensor(tail_scaled[c], score_ps[:, c, :], mod[:, 1, E:], ALU.mult).then_inc(tail_scaled_ready, 1)

            def tail_residual(c):
                dve.wait_ge(tail_rstd, c // 2 + 1)
                dve.wait_ge(tail_shifted, c + 1)
                dve.scalar_tensor_tensor(tail_x[c], tail_scaled[c], tail_inv_rms[:, c:c + 1], tail_x[c],
                                         ALU.mult, ALU.add).then_inc(tail_summed, 1)

            dve.wait_ge(summed, TC * (B - 1))
            dve.wait_ge(stored[1], 16 * (TC * (B - 1) // 2 - 1))
            rotate(0, x_s[:, 1], acc[:, 1])
            for c in (0, 1):
                tail_rescale(c)
            dve.wait_ge(tail_scaled_ready, 2)
            for c in (1, 0):
                tail_residual(c)
            dve.wait_ge(tail_summed, 2)
            rotate(1, tail_x[0], tail_out[0])
            for c in (2, 3):
                tail_rescale(c)
            dve.wait_ge(tail_scaled_ready, 4)
            for c in (2, 3):
                tail_residual(c)
            dve.wait_ge(tail_summed, 4)
            for c in (2, 3):
                rotate(c, tail_x[c], tail_out[c])

        @block.scalar
        def _(act):
            def exp(n, s, r):
                act.wait_ge(masked, TILES * n + r + 1)
                if r == 0 and not known(n, 2):
                    act.wait_ge(inverted, n - 1)
                act.activation(probs[:, s % 2, r, :], probs[:, s % 2, r, :], ACT.Exp, bias=least[:, s % 2, r:r + 1],
                               scale=-1.0, accum_out=den[:, s % 2, r:r + 1]).then_inc(exped, 1)

            def move_out(n, s, r):
                act.wait_ge(turned, TILES * n + r + 1)
                if not known(n, 2):
                    act.wait_ge(valued, n - 1)
                act.activation(probs_T[:, s % 2, r // 2, 2 * (r % 2):2 * (r % 2) + 2, :],
                               prob_ps[:, r % 2, :].rearrange("p (j t) -> p j t", j=2), ACT.Copy).then_inc(out_act, 1)

            def values_out(n, s):
                act.wait_ge(valued, n + 1)
                act.wait_ge(scale_turned, n + 1)
                if not known(n, 2):
                    act.wait_ge(o_scaled, n - 1)
                act.activation(raw_T[:, s % 2], out_ps[:, :, :], ACT.Copy).then_inc(raw_out, 1)

            def square(b, p, c):
                m = TC * b + c
                act.wait_ge(y_ready, m + 1)
                if not known(m, 1):
                    act.wait_ge(squared, m)
                if not known(m, 2):
                    act.wait_ge(mean_ready, m - 1)
                act.activation(junk[:, :], y_ps[:, :], ACT.Square,
                               accum_out=sum_sq[:, c % 2:c % 2 + 1]).then_inc(squared, 1)

            def batch(b, p, first=False, last=False):
                for s in range(STEPS):
                    n = STEPS * b + s
                    for r in range(TILES):
                        if not (last and s == STEPS - 1):
                            exp(n + 1, s + 1, r)
                        if r >= 1 and r - 1 in BY_ACT[s % 2]:
                            move_out(n, s, r - 1)
                        if r == VALUES_OUT_AT and not (first and s == 0):
                            values_out(n - 1, s - 1)
                        if r == SQUARE_AT and chunk_before(b, p, s):
                            square(*chunk_before(b, p, s))
                    if TILES - 1 in BY_ACT[s % 2]:
                        move_out(n, s, TILES - 1)

            for r in range(TILES):
                exp(0, 0, r)
            batch(0, 0, first=True)
            batch(1, 1)
            with act.Fori(2, B - 3, 2) as b:
                batch(b, 0)
                batch(b + 1, 1)
            batch(B - 2, 0)
            batch(B - 1, 1, last=True)
            values_out(STEPS * B - 1, STEPS - 1)
            square(B - 2, 0, TC - 1)
            for c in range(TC):
                act.wait_ge(y_ready, TC * (B - 1) + c + 1)
                if c == 0:
                    act.wait_ge(squared, TC * (B - 1))
                else:
                    act.wait_ge(tail_squared, c)
                act.activation(junk[:, :], score_ps[:, c, :], ACT.Square,
                               accum_out=tail_sum_sq[:, c:c + 1]).then_inc(tail_squared, 1)

        @block.gpsimd
        def _(pool):
            def split(b, p, s):
                n = STEPS * b + s
                g, half = s // 2, s % 2
                t = slice(half * HALF, (half + 1) * HALF)
                if s == 0 and not known(b, 2):
                    pool.wait_ge(y_ready, TC * (b - 1))
                pool.wait_ge(raw_out, n + 1)
                if not known(n, 2):
                    pool.wait_ge(o_ready, n - 1)
                pool.tensor_tensor(o_T[:, s % 2], raw_T[:, s % 2, 0], raw_T[:, s % 2, 1], ALU.mult).then_inc(o_scaled, 1)
                pool.wait_ge(o_scaled, n + 1)
                take_waits(pool)
                pool.tensor_copy(o_hi[:, p, g, t], o_T[:, s % 2]).then_inc(o_hi_ready, 1)
                pool.wait_ge(o_hi_ready, n + 1)
                pool.tensor_tensor(o_lo[:, p, g, t], o_T[:, s % 2], f32(o_hi[:, p, g, t]),
                                   ALU.subtract).then_inc(o_ready, 1)

            def shift(b, p, c):
                m = TC * b + c
                if c == 0:
                    pool.wait_ge(mod_in[p], 8 * (b - p) + 16)
                pool.wait_ge(x_in[c % 2], 16 * (2 * b + c // 2 + 1))
                pool.tensor_tensor(x_s[:, c % 2], x_s[:, c % 2], mod[:, p, 0:E], ALU.add).then_inc(shifted, 1)

            def rms(b, p, c):
                m = TC * b + c
                pool.wait_ge(squared, m + 1)
                take_waits(pool)
                pool.tensor_scalar(mean_sq[:, c % 2:c % 2 + 1], sum_sq[:, c % 2:c % 2 + 1], 1.0 / E, RMS_EPS,
                                   ALU.mult, ALU.add).then_inc(mean_ready, 1)
                pool.wait_ge(mean_ready, m + 1)
                if not known(m, 2):
                    pool.wait_ge(summed, m - 1)
                pool.tensor_tensor(rstd[:, c % 2:c % 2 + 1], mean_sq[:, c % 2:c % 2 + 1], neg_half[:, :],
                                   ALU.pow).then_inc(rstd_ready, 1)

            def rotate(b, p, c):
                m = TC * b + c
                pool.wait_ge(summed, m + 1)
                if not known(m, 2):
                    pool.wait_ge(stored[c % 2], 16 * (2 * b + c // 2))
                if not known(m, 1):
                    pool.wait_ge(rotated, m)
                rotation_products(pool, mix, x_s[:, c % 2]).then_inc(mixing, 1)
                pool.wait_ge(mixing, m + 1)
                pool.tensor_tensor(mix[:, 0:2, :], mix[:, 0:2, :], mix[:, 2:4, :], ALU.add).then_inc(paired, 1)
                pool.wait_ge(paired, m + 1)
                pool.tensor_tensor(acc[:, c % 2], mix[:, 0, :], mix[:, 1, :], ALU.add).then_inc(rotated, 1)

            def batch(b, p, first=False):
                for s in range(STEPS):
                    if s % 2 == 0 and not first:
                        shift(b - 1, 1 - p, s // 2)
                    if chunk_before(b, p, s):
                        rms(*chunk_before(b, p, s))
                    if s % 2 == 1 and chunk_before(b, p, s - 1):
                        rotate(*chunk_before(b, p, s - 1))
                    if s > 0:
                        split(b, p, s - 1)
                    elif not first:
                        split(b - 1, 1 - p, STEPS - 1)

            pool.memset(neg_half[:, :], -0.5).then_inc(half_set, 1)
            pool.wait_ge(half_set, 1)
            batch(0, 0, first=True)
            batch(1, 1)
            with pool.Fori(2, B - 3, 2) as b:
                batch(b, 0)
                batch(b + 1, 1)
            batch(B - 2, 0)
            batch(B - 1, 1)
            rms(B - 2, 0, TC - 1)
            split(B - 1, 1, STEPS - 1)
            pool.wait_ge(mod_in[1], 16 * (B // 2))
            for c in range(TC):
                pool.wait_ge(tail_in[c], 16)
                pool.tensor_tensor(tail_x[c], tail_x[c], mod[:, 1, 0:E], ALU.add).then_inc(tail_shifted, 1)
            for pair in range(2):
                cols = slice(2 * pair, 2 * pair + 2)
                pool.wait_ge(tail_squared, 2 * pair + 2)
                pool.tensor_scalar(tail_mean_sq[:, cols], tail_sum_sq[:, cols], 1.0 / E, RMS_EPS,
                                   ALU.mult, ALU.add).then_inc(tail_mean, 1)
                pool.wait_ge(tail_mean, pair + 1)
                pool.tensor_tensor(tail_inv_rms[:, cols], tail_mean_sq[:, cols],
                                   neg_half[:, :].to_broadcast([P, 2]), ALU.pow).then_inc(tail_rstd, 1)
            pool.wait_ge(tail_summed, 1)
            pool.wait_ge(rotated, TC * (B - 1) - 1)
            rotation_products(pool, mix, tail_x[BY_POOL]).then_inc(mixing, 1)
            pool.wait_ge(mixing, TC * (B - 1))
            pool.tensor_tensor(mix[:, 0:2, :], mix[:, 0:2, :], mix[:, 2:4, :], ALU.add).then_inc(paired, 1)
            pool.wait_ge(paired, TC * (B - 1))
            pool.wait_ge(turned, ALL_TURNED)
            pool.tensor_tensor(tail_out[BY_POOL], mix[:, 0, :], mix[:, 1, :], ALU.add).then_inc(rotated, 1)


def program(nc, x, xT, cond, condT, mask, wT, rms_scale, wcT, bc, q_right, gate, out):
    scr = {n: nc.dram_tensor(f"{n}_scratch", (B * NG, 2, P, S), F32, kind="Internal").ap() for n in "qk"}
    scr["v"] = nc.dram_tensor("v_scratch", (B, TC, P, E), F32, kind="Internal").ap()
    mod_scr = nc.dram_tensor("mod_scratch", (B, 2 * E), F32, kind="Internal").ap()
    with ExitStack() as ctx:
        wo_hi = ctx.enter_context(nc.sbuf_tensor("wo_hi", [P, KC, E], F32R))
        wo_lo = ctx.enter_context(nc.sbuf_tensor("wo_lo", [P, KC, E], F32R))
        mask_bias = ctx.enter_context(nc.sbuf_tensor("mask_bias", [P, TC, S], BF16))
        rot = ctx.enter_context(nc.sbuf_tensor("rot", [P, 4, 4, C], F32))
        ident = ctx.enter_context(nc.sbuf_tensor("ident", [P, P], F32))
        projections(nc, xT, wT, scr, wo_hi, wo_lo, mask, condT, cond, wcT, bc, rms_scale, q_right, gate, mod_scr,
                    mask_bias, rot, ident)
        attention(nc, x, scr, mod_scr, out, mask_bias, rot, ident, wo_hi, wo_lo)


def kernel(**inputs):
    import numpy as np
    import concourse.bacc as bacc
    from concourse.bass_utils import run_bass_kernel_spmd

    def laid(a):
        return np.ascontiguousarray(a)

    nc = bacc.Bacc("TRN2", target_bir_lowering=False, num_devices=1)
    x, cond = np.asarray(inputs["x"]), np.asarray(inputs["cond_256"])
    arrays = {
        "x": laid(x),
        "xT": laid(x.transpose(0, 2, 1)),
        "cond": laid(cond.reshape(-1)),
        "condT": laid(cond.T),
        "mask": laid(np.asarray(inputs["mask_SxS_bk1"]).view(np.int32)),
        "wqT": laid(np.asarray(inputs["L0_cond_Wq"]).T),
        "wkT": laid(np.asarray(inputs["L0_cond_Wk"]).T),
        "wvT": laid(np.asarray(inputs["L0_cond_Wv"]).T),
        "woT": laid(np.asarray(inputs["L0_cond_Wo"]).T),
        "rms_scale": laid(inputs["L0_cond_rms_scale"]),
        "wcT": laid(np.asarray(inputs["L0_cond_Wc"]).T),
        "bc": laid(inputs["L0_cond_bc"]),
        "q_right": laid(np.asarray(inputs["L1_cond_q_right"]).reshape(-1)),
        "gate": laid(np.asarray(inputs["L1_cond_spectral_gate"]).reshape(-1)),
    }
    dram = {n: nc.dram_tensor(f"in_{n}", a.shape, mybir.dt.from_np(a.dtype), kind="ExternalInput").ap()
            for n, a in arrays.items()}
    out = nc.dram_tensor("out_0", (B, S, E), F32, kind="ExternalOutput").ap()
    program(nc, dram["x"], dram["xT"], dram["cond"], dram["condT"], dram["mask"],
            [dram["wqT"], dram["wkT"], dram["wvT"], dram["woT"]], dram["rms_scale"], dram["wcT"], dram["bc"],
            dram["q_right"], dram["gate"], out)
    r = run_bass_kernel_spmd(nc, [{f"in_{n}": a for n, a in arrays.items()}], core_ids=[0])
    return r.results[0]["out_0"]
```

```python
from contextlib import ExitStack

import concourse.bass as bass
from concourse import mybir

ALU = mybir.AluOpType
ACT = mybir.ActivationFunctionType
AX_X = mybir.AxisListType.X
F32 = mybir.dt.float32
F32R = mybir.dt.float32r
BF16 = mybir.dt.bfloat16
U8 = mybir.dt.uint8

P = 128
B, S, E = 8, 512, 512
H, D = 16, 32
C = 128
KC = E // P
TC = S // P
HG = P // D
NG = H // HG
HALF = S // 2
STEPS = 2 * NG
TILES = 2 * HG
MASKED = 1e30
QSCALE = -float(D) ** -0.5
RMS_EPS, NORM_EPS = 1e-6, 1e-8


def f32(ap):
    return ap.bitcast(F32)


class Rows:

    def __init__(self, nc, ctx, scr):
        self.q = ctx.enter_context(nc.sbuf_tensor("q_rows", [P, 2, HG, S], F32R))
        self.k = ctx.enter_context(nc.sbuf_tensor("k_rows", [P, 2, HG, S], F32R))
        self.q_in = [ctx.enter_context(nc.semaphore(f"q_in{i}")) for i in range(2)]
        self.k_in = [ctx.enter_context(nc.semaphore(f"k_in{i}")) for i in range(2)]
        self.scr = scr

    def load(self, sp, u, g):
        p = g % 2
        for r in range(4):
            rows = slice(r * D, (r + 1) * D)
            sp.dma_start(f32(self.q[rows, p]),
                         self.scr["q"][u, r % 2].rearrange("(i d) t -> d i t", d=D)).then_inc(self.q_in[p], 16)
            sp.dma_start(f32(self.k[rows, p]),
                         self.scr["k"][u, r // 2].rearrange("(i d) t -> d i t", d=D)).then_inc(self.k_in[p], 16)


def projections(nc, xT, wT, scr, raw, rows, late, qk_stored, wo_hi, wo_lo, mask, condT, cond, wcT, bc, rms_scale,
                q_right, gate, mod_scr, mask_bias, rot, ident):
    with ExitStack() as ctx:
        def sb(name, shape, dt):
            return ctx.enter_context(nc.sbuf_tensor(name, shape, dt))

        def sem(name):
            return ctx.enter_context(nc.semaphore(name))

        x_raw = [raw[:, 0], raw[:, 1]]
        w_raw = [raw[:, 2], raw[:, 3]]
        w_hi = [sb(f"w_hi_{n}", [P, KC, E], F32R) for n in "qkv"] + [wo_hi]
        w_lo = [sb(f"w_lo_{n}", [P, KC, E], F32R) for n in "qkv"] + [wo_lo]
        x_hi = sb("x_hi", [P, 2, KC, S], F32R)
        x_lo = sb("x_lo", [P, 2, KC, S], F32R)
        qk_hi = [late[:, j, :].bitcast(F32R) for j in range(4)]
        qk_lo = [late[:, 4 + j, :].bitcast(F32R) for j in range(4)]
        v_out = sb("v_out", [P, 4, E], F32)
        proj = ctx.enter_context(nc.psum_tensor("proj", [P, 4, 512], F32))

        mask_words = sb("mask_words", [P, TC, S // 4], mybir.dt.int32)
        mask_u8 = mask_words[:, :, :].bitcast(U8)
        row_least = sb("row_least", [P, TC], F32)
        row_open = sb("row_open", [P, TC], F32)
        row_nan = sb("row_nan", [P, TC], F32)
        nan_part = sb("nan_part", [P, 1], F32)
        ones8 = sb("ones8", [P, B], F32)
        nan_all = sb("nan_all", [B, 1], F32)
        cT = sb("cT", [P, B], F32)
        c_sig = sb("c_sig", [P, B], F32)
        c_silu = sb("c_silu", [P, B], F32)
        wc = sb("wc", [P, 2 * E], F32)
        bc8 = sb("bc8", [B, 2 * E], F32)
        rms8 = sb("rms8", [B, E], F32)
        mod = sb("mod", [B, 2 * E], F32)
        quat = sb("quat", [P, 12, C], F32)
        square = sb("square", [P, 12, C], F32)
        neg_half = sb("neg_half", [P, 2, C], F32)
        gate_b = sb("gate_b", [P, C], F32)
        term = sb("term", [P, 4, 4, C], F32)
        left = w_raw[0].rearrange("p k (i d) -> p k i d", i=4)
        right = w_raw[1].rearrange("p k (j d) -> p k j d", j=4)
        mod_ps = ctx.enter_context(nc.psum_tensor("mod_ps", [P, 3, 512], F32))

        loaded = sem("loaded")
        pool_step, dve_step = sem("pool_step"), sem("dve_step")
        sig_exp, silu_ready = sem("sig_exp"), sem("silu_ready")
        nan_ready = sem("nan_ready")
        mod_matmul = sem("mod_matmul")
        mod_ready, mod_stored = sem("mod_ready"), sem("mod_stored")
        rot_ready = sem("rot_ready")

        w_in = [sem(f"w_in{i}") for i in range(2)]
        x_in = [sem(f"x_in{i}") for i in range(2)]
        first_in = [sem(f"first_in{k}") for k in range(KC)]
        first_hi, first_lo = sem("first_hi"), sem("first_lo")
        w_hi_ready, w_lo_ready = sem("w_hi_ready"), sem("w_lo_ready")
        x_hi_ready, x_lo_ready = sem("x_hi_ready"), sem("x_lo_ready")
        projected = sem("projected")
        v_copied = sem("v_copied")
        qk_hi_ready, qk_lo_ready = sem("qk_hi_ready"), sem("qk_lo_ready")
        v_stored = [sem(f"v_stored{i}") for i in range(4)]

        VT, QKT = TC, 2 * NG
        TASKS = VT + QKT
        W_ORDER = (2, 0, 1, 3)
        LOADED = 16 * 8

        block = ctx.enter_context(nc.Block())

        @block.sync
        def _(sp):
            def load_x(b, p):
                sp.dma_start(x_raw[p], xT[b].rearrange("(k p) t -> p k t", p=P)).then_inc(x_in[p], 16)

            def load_w(n):
                sp.dma_start(w_raw[n % 2], wT[W_ORDER[n]].rearrange("(k p) e -> p k e", p=P)).then_inc(w_in[n % 2], 16)

            for k in range(KC):
                sp.dma_start(w_raw[0][:, k], wT[W_ORDER[0]][k * P:(k + 1) * P, :]).then_inc(first_in[k], 16)
                sp.dma_start(x_raw[0][:, k], xT[0, k * P:(k + 1) * P, :]).then_inc(first_in[k], 16)
            load_w(1)
            sp.wait_ge(first_lo, 2 * KC)
            load_w(2)
            sp.dma_start(mask_words[:, :, :], mask.rearrange("(c p) t -> p c t", p=P)).then_inc(loaded, 16)
            sp.dma_start(cT[:, :], condT).then_inc(loaded, 16)
            sp.dma_start(quat[:, 0:8, :], cond.partition_broadcast(P)).then_inc(loaded, 16)
            sp.dma_start(quat[:, 8:12, :], q_right.partition_broadcast(P)).then_inc(loaded, 16)
            sp.dma_start(gate_b[:, :], gate.partition_broadcast(P)).then_inc(loaded, 16)
            sp.dma_start(wc[:, :], wcT).then_inc(loaded, 16)
            sp.dma_start(bc8[:, :], bc.partition_broadcast(B)).then_inc(loaded, 16)
            sp.dma_start(rms8[:, :], rms_scale.partition_broadcast(B)).then_inc(loaded, 16)
            load_x(1, 1)
            sp.wait_ge(w_lo_ready, 1)
            load_w(3)

            def store_v(b, c):
                sp.wait_ge(v_copied, VT * b + c + 1)
                sp.dma_start(scr["v"][b, c], v_out[:, c, :]).then_inc(v_stored[c], 16)

            def store_qk(b, which, g):
                sp.wait_ge(qk_lo_ready, QKT * b + NG * which + g + 1)
                to = scr["qk"[which]][b * NG + g]
                sp.dma_start(to[0], late[:, g, :]).then_inc(qk_stored[g], 16)
                sp.dma_start(to[1], late[:, 4 + g, :]).then_inc(qk_stored[g], 16)

            def batch(b, p, more, last=False):
                for c in range(TC):
                    store_v(b, c)
                if last:
                    sp.wait_ge(mod_ready, 1)
                    sp.dma_start(mod_scr, mod[:, :]).then_inc(mod_stored, 16)
                    sp.wait_ge(x_lo_ready, B - 1)
                    sp.wait_ge(rot_ready, 1)
                    for g in range(2):
                        sp.wait_ge(qk_stored[g], 64)
                        rows.load(sp, g, g)
                if more:
                    if not (isinstance(b, int) and b == 0):
                        sp.wait_ge(x_lo_ready, b)
                    load_x(b + 2, p)
                for which in range(2):
                    for g in range(NG):
                        store_qk(b, which, g)

            batch(0, 0, True)
            batch(1, 1, True)
            with sp.Fori(2, B - 3, 2) as b:
                batch(b, 0, True)
                batch(b + 1, 1, True)
            batch(B - 2, 0, False)
            batch(B - 1, 1, False, last=True)
            sp.wait_ge(mod_stored, 16)
            for c in range(TC):
                sp.wait_ge(v_stored[c], 16 * B)

        @block.scalar
        def _(act):
            def split_w(n):
                act.wait_ge(w_in[n % 2], 16 * (n // 2 + n % 2))
                act.activation(w_hi[W_ORDER[n]][:, :, :], w_raw[n % 2], ACT.Copy).then_inc(w_hi_ready, 1)

            def split_x(b, p):
                act.wait_ge(x_in[p], 8 * (b + p))
                if not (isinstance(b, int) and b < 2):
                    act.wait_ge(projected, TASKS * (b - 1))
                act.activation(x_hi[:, p], x_raw[p], ACT.Copy).then_inc(x_hi_ready, 1)

            def batch(b, p, more, first=False):
                for c in range(VT):
                    act.wait_ge(projected, TASKS * b + c + 1)
                    if not first:
                        act.wait_ge(v_stored[c], 16 * b)
                    act.activation(v_out[:, c, :], proj[:, c, :], ACT.Copy).then_inc(v_copied, 1)
                if first:
                    act.wait_ge(loaded, LOADED)
                    act.activation(c_sig[:, :], cT[:, :], ACT.Exp, scale=-1.0).then_inc(sig_exp, 1)
                for m in range(QKT):
                    act.wait_ge(projected, TASKS * b + VT + m + 1)
                    if not (first and m < 4):
                        act.wait_ge(qk_stored[m % 4], 64 * b + 32 * (m // 4))
                    act.activation(qk_hi[m % 4], proj[:, m % 4, :], ACT.Copy,
                                   scale=QSCALE if m < NG else 1.0).then_inc(qk_hi_ready, 1)
                    if m == 1 and more:
                        split_x(b + 1, 1 - p)

            for k in range(KC):
                act.wait_ge(first_in[k], 32)
                act.activation(w_hi[2][:, k], w_raw[0][:, k], ACT.Copy).then_inc(first_hi, 1)
                act.activation(x_hi[:, 0, k], x_raw[0][:, k], ACT.Copy).then_inc(first_hi, 1)
            for n in (1, 2):
                split_w(n)
            batch(0, 0, True, first=True)
            with act.Fori(1, B - 2, 2) as b:
                batch(b, 1, True)
                batch(b + 1, 0, True)
            batch(B - 1, 1, False)

        @block.vector
        def _(dve):
            def split_w(n):
                dve.wait_ge(w_hi_ready, n)
                dve.tensor_tensor(w_lo[W_ORDER[n]][:, :, :], w_raw[n % 2], f32(w_hi[W_ORDER[n]][:, :, :]),
                                  ALU.subtract).then_inc(w_lo_ready, 1)

            def split_x(b, p):
                dve.wait_ge(x_hi_ready, b)
                dve.tensor_tensor(x_lo[:, p], x_raw[p], f32(x_hi[:, p]), ALU.subtract).then_inc(x_lo_ready, 1)

            def batch(b, p, more):
                for m in range(QKT):
                    dve.wait_ge(qk_hi_ready, QKT * b + m + 1)
                    dve.scalar_tensor_tensor(qk_lo[m % 4], proj[:, m % 4, :], QSCALE if m < NG else 1.0,
                                             late[:, m % 4, :], ALU.mult, ALU.subtract).then_inc(qk_lo_ready, 1)
                    if m == 1 and more:
                        split_x(b + 1, 1 - p)

            for k in range(KC):
                dve.wait_ge(first_hi, 2 * k + 1)
                dve.tensor_tensor(w_lo[2][:, k], w_raw[0][:, k], f32(w_hi[2][:, k]), ALU.subtract).then_inc(first_lo, 1)
                dve.wait_ge(first_hi, 2 * k + 2)
                dve.tensor_tensor(x_lo[:, 0, k], x_raw[0][:, k], f32(x_hi[:, 0, k]), ALU.subtract).then_inc(first_lo, 1)
            for n in (1, 2):
                split_w(n)

            done = [0]

            def link(ins):
                done[0] += 1
                ins.then_inc(dve_step, 1)
                dve.wait_ge(dve_step, done[0])

            dve.wait_ge(loaded, LOADED)
            link(dve.tensor_scalar(mask_bias[:, :, :], mask_u8, MASKED, None, ALU.mult))
            link(dve.tensor_reduce(row_least[:, :], mask_bias[:, :, :], AX_X, ALU.min))
            link(dve.tensor_scalar(row_open[:, :], row_least[:, :], MASKED / 2, None, ALU.is_lt))
            link(dve.reciprocal(row_nan[:, :], row_open[:, :]))
            link(dve.tensor_scalar(row_nan[:, :], row_nan[:, :], 0.0, None, ALU.mult))
            dve.tensor_reduce(nan_part[:, :], row_nan[:, :], AX_X, ALU.add).then_inc(nan_ready, 1)
            dve.wait_ge(sig_exp, 1)
            link(dve.tensor_scalar(c_sig[:, :], c_sig[:, :], 1.0, None, ALU.add))
            link(dve.reciprocal(c_sig[:, :], c_sig[:, :]))
            dve.tensor_tensor(c_silu[:, :], cT[:, :], c_sig[:, :], ALU.mult).then_inc(silu_ready, 1)

            with dve.Fori(0, B - 3, 2) as b:
                batch(b, 0, True)
                batch(b + 1, 1, True)
            dve.wait_ge(mod_matmul, 3)
            link(dve.tensor_copy(nan_all[:, :], mod_ps[0:B, 2, 0:1]))
            link(dve.scalar_tensor_tensor(mod[:, 0:E], mod_ps[0:B, 0, :], nan_all[:, 0:1], bc8[:, 0:E],
                                          ALU.add, ALU.add))
            link(dve.tensor_tensor(mod[:, E:], mod_ps[0:B, 1, :], bc8[:, E:], ALU.add))
            dve.scalar_tensor_tensor(mod[:, E:], mod[:, E:], 1.0, rms8[:, :], ALU.add, ALU.mult).then_inc(mod_ready, 1)
            batch(B - 2, 0, True)
            batch(B - 1, 1, False)

        @block.tensor
        def _(pe):
            def passes(out, hi, lo, other_hi, other_lo, first=False):
                for k in range(KC):
                    if first:
                        pe.wait_ge(first_lo, 2 * k + 2)
                    pe.matmul(out, hi(k), other_hi(k), start=(k == 0), stop=False)
                    pe.matmul(out, hi(k), other_lo(k), start=False, stop=False)
                    last = pe.matmul(out, lo(k), other_hi(k), start=False, stop=(k == KC - 1))
                last.then_inc(projected, 1)

            def batch(b, p, first=False):
                for c in range(VT):
                    if c == 0 and not first:
                        pe.wait_ge(x_lo_ready, b)
                    if not first:
                        pe.wait_ge(qk_lo_ready, QKT * b - 4 + c + 1)
                    t = slice(c * P, (c + 1) * P)
                    passes(proj[:, c, :], lambda k: x_hi[:, p, k, t], lambda k: x_lo[:, p, k, t],
                           lambda k: w_hi[2][:, k, :], lambda k: w_lo[2][:, k, :],
                           first=first and c == 0)
                for m in range(QKT):
                    if m < 4:
                        pe.wait_ge(v_copied, VT * b + m + 1)
                    else:
                        pe.wait_ge(qk_lo_ready, QKT * b + m - 3)
                    w = m // NG
                    if first and m % NG == 0:
                        pe.wait_ge(w_lo_ready, 1 + w)
                    e = slice((m % NG) * P, (m % NG + 1) * P)
                    passes(proj[:, m % 4, :], lambda k: w_hi[w][:, k, e], lambda k: w_lo[w][:, k, e],
                           lambda k: x_hi[:, p, k, :], lambda k: x_lo[:, p, k, :])

            batch(0, 0, first=True)
            pe.wait_ge(silu_ready, 1)
            pe.wait_ge(nan_ready, 2)
            for h in range(2):
                pe.matmul(mod_ps[0:B, h, :], c_silu[:, :], wc[:, h * E:(h + 1) * E],
                          start=True, stop=True).then_inc(mod_matmul, 1)
            pe.matmul(mod_ps[0:B, 2, 0:1], ones8[:, :], nan_part[:, :], start=True, stop=True).then_inc(mod_matmul, 1)
            with pe.Fori(1, B - 2, 2) as b:
                batch(b, 1)
                batch(b + 1, 0)
            batch(B - 1, 1)

        @block.gpsimd
        def _(pool):
            done = [0]

            def link(ins):
                done[0] += 1
                ins.then_inc(pool_step, 1)
                pool.wait_ge(pool_step, done[0])

            pool.memset(ones8[:, :], 1.0).then_inc(nan_ready, 1)
            pool.memset(neg_half[:, :, :], -0.5)
            link(pool.memset(ident[:, :], 0.0))
            link(pool.affine_select(out=ident[:, :], in_=ident[:, :], compare_op=ALU.not_equal, fill=1.0,
                                    base=0, pattern=[[-1, P]], channel_multiplier=1))
            pool.wait_ge(loaded, LOADED)
            link(pool.tensor_tensor(square[:, :, :], quat[:, :, :], quat[:, :, :], ALU.mult))
            link(pool.tensor_tensor(square[:, 0:4, :], square[:, 0:4, :], square[:, 4:8, :], ALU.add))
            pool.tensor_tensor(square[:, 4:6, :], square[:, 0:2, :], square[:, 2:4, :], ALU.add)
            link(pool.tensor_tensor(square[:, 6:8, :], square[:, 8:10, :], square[:, 10:12, :], ALU.add))
            sums = square[:, 4:8, :].rearrange("p (q h) d -> p q h d", h=2)
            link(pool.tensor_tensor(square[:, 0:2, :], sums[:, :, 0, :], sums[:, :, 1, :], ALU.add))
            link(pool.tensor_scalar(square[:, 0:2, :], square[:, 0:2, :], 1.0, NORM_EPS, ALU.mult, ALU.add))
            link(pool.tensor_tensor(square[:, 2:4, :], square[:, 0:2, :], neg_half[:, :, :], ALU.pow))
            pool.tensor_tensor(quat[:, 0:4, :], quat[:, 0:4, :],
                               square[:, 2, :].unsqueeze(1).to_broadcast([P, 4, C]), ALU.mult)
            link(pool.tensor_tensor(square[:, 8, :], square[:, 3, :], gate_b[:, :], ALU.mult))
            link(pool.tensor_tensor(quat[:, 8:12, :], quat[:, 8:12, :],
                                    square[:, 8, :].unsqueeze(1).to_broadcast([P, 4, C]), ALU.mult))
            by_left = [[(0, 1), (1, -1), (2, -1), (3, -1)], [(1, 1), (0, 1), (3, -1), (2, 1)],
                       [(2, 1), (3, 1), (0, 1), (1, -1)], [(3, 1), (2, -1), (1, 1), (0, 1)]]
            by_right = [[(0, 1), (1, 1), (2, 1), (3, 1)], [(1, -1), (0, 1), (3, -1), (2, 1)],
                        [(2, -1), (3, 1), (0, 1), (1, -1)], [(3, -1), (2, -1), (1, 1), (0, 1)]]
            pool.wait_ge(w_in[1], 32)
            link(pool.tensor_copy(w_hi[3][:, :, :], w_raw[1]))
            link(pool.tensor_tensor(w_lo[3][:, :, :], w_raw[1], f32(w_hi[3][:, :, :]), ALU.subtract))
            pool.wait_ge(w_lo_ready, 2)
            for i in range(4):
                for k in range(4):
                    q, sign = by_left[i][k]
                    pool.tensor_scalar(left[:, k, i, :], quat[:, q, :], float(sign), 0.0, ALU.mult, ALU.add)
            for k in range(4):
                for j in range(4):
                    q, sign = by_right[k][j]
                    last = pool.tensor_scalar(right[:, k, j, :], quat[:, 8 + q, :], float(sign), 0.0, ALU.mult, ALU.add)
            link(last)

            for k in range(4):
                to = rot if k == 0 else term
                for j in range(4):
                    last = pool.tensor_tensor(to[:, j], left[:, k], right[:, k, j, :].unsqueeze(1).to_broadcast([P, 4, C]),
                                              ALU.mult)
                link(last)
                if k > 0:
                    link(pool.tensor_tensor(rot[:, :, :, :], rot[:, :, :, :], term[:, :, :, :], ALU.add))
            for i in range(4):
                last = pool.tensor_scalar(rot[:, i, i, :], rot[:, i, i, :], 1.0, 1.0, ALU.mult, ALU.add)
            last.then_inc(rot_ready, 1)


def attention(nc, x, scr, rows, late, qk_stored, mod_scr, out, mask_bias, rot, ident, wo_hi, wo_lo):
    with ExitStack() as ctx:
        def sb(name, shape, dt=F32):
            return ctx.enter_context(nc.sbuf_tensor(name, shape, dt))

        def ps(name, shape):
            return ctx.enter_context(nc.psum_tensor(name, shape, F32))

        def sem(name):
            return ctx.enter_context(nc.semaphore(name))

        v_sb = sb("v_sb", [P, 2, TC, E], F32)
        probs = sb("probs", [P, 2, TILES, S])
        den = sb("den", [P, 2, TILES])
        least = sb("least", [P, 2, TILES])
        inv_sum = sb("inv_sum", [P, 2, HG])
        inv_den = sb("inv_den", [P, 2, HG, D])
        probs_T = sb("probs_T", [P, 2, HG, TC, HALF])
        raw_T = sb("raw_T", [P, 2, 2, HALF])
        o_T = sb("o_T", [P, 2, HALF])
        o_hi = sb("o_hi", [P, 2, NG, S], F32R)
        o_lo = sb("o_lo", [P, 2, NG, S], F32R)
        mod = sb("mod_b", [P, 2, 2 * E])
        x_s = late[:, 4:6, :]
        scaled = sb("scaled", [P, E])
        junk = sb("junk", [P, E], BF16)
        sum_sq = sb("sum_sq", [P, 2])
        mean_sq = sb("mean_sq", [P, 2])
        rstd = sb("rstd", [P, 2])
        tail_sum_sq = sb("tail_sum_sq", [P, TC])
        tail_mean_sq = sb("tail_mean_sq", [P, TC])
        tail_inv_rms = sb("tail_inv_rms", [P, TC])
        neg_half = sb("minus_half", [P, 1])
        mix = late[:, 0:4, :]
        acc = late[:, 6:8, :]

        score_ps = ps("score_ps", [P, 4, 512])
        prob_ps = ps("prob_ps", [P, 2, 512])
        out_ps = ps("out_ps", [P, 2, HALF])
        value_ps, scale_ps = out_ps[:, 0, :], out_ps[:, 1, :]
        y_ps = ps("y_ps", [P, 512])

        v_in = [sem(f"v_in{i}") for i in range(2)]
        mod_in = [sem(f"mod_in{i}") for i in range(2)]
        x_in = [sem(f"xc_in{i}") for i in range(2)]
        stored = [sem(f"stored{i}") for i in range(2)]
        scores = sem("scores")
        masked = sem("masked")
        exped = sem("exped")
        inv_sum_ready = sem("inv_sum_ready")
        inverted = sem("inverted")
        turned = sem("turned")
        out_act, out_dve = sem("out_act"), sem("out_dve")
        scale_turned = sem("scale_turned")
        valued = sem("valued")
        raw_out = sem("raw_out")
        o_scaled = sem("o_scaled")
        o_hi_ready, o_ready = sem("o_hi_ready"), sem("o_ready")
        y_ready = sem("y_ready")
        squared = sem("squared")
        mean_ready, rstd_ready = sem("mean_ready"), sem("rstd_ready")
        scaled_ready = sem("scaled_ready")
        shifted = sem("shifted")
        summed = sem("summed")
        half_set = sem("half_set")
        passed = sem("passed")
        mixing = sem("mixing")
        paired = sem("paired")
        rotated = sem("rotated")

        SCORE_AHEAD, MASK_AHEAD = 3, 2
        PROJECT_AT, VALUE_AT = (0, 1), (2, 3, 4, 5)
        TURN_SCALE_AT = 6
        VALUES_OUT_AT, SQUARE_AT = 6, 2
        INVERT_AT, RESCALE_AT, RESIDUAL_AT = 7, 4, 2
        BY_ACT = (1, 3, 5, 7)
        BY_DVE = tuple(r for r in range(TILES) if r not in BY_ACT)

        def moved_out(eng, n, r):
            if r in BY_ACT:
                eng.wait_ge(out_act, len(BY_ACT) * n + BY_ACT.index(r) + 1)
            else:
                eng.wait_ge(out_dve, len(BY_DVE) * n + BY_DVE.index(r) + 1)

        def take_waits(eng):
            eng.sem_inc(passed, 1)

        def known(v, least_value):
            return isinstance(v, int) and v < least_value

        def rotation_products(eng, to, chunk):
            return eng.tensor_tensor(to.rearrange("p j (i d) -> p j i d", i=4), rot[:, :, :, :],
                                     chunk.rearrange("p (j d) -> p j d", j=4).unsqueeze(2).to_broadcast([P, 4, 4, C]),
                                     ALU.mult)

        def tile_ahead(b, s, r, last):
            s, r = s + 1 + r // TILES, r % TILES
            if s < STEPS:
                return b, s, r
            return None if last else (b + 1, s - STEPS, r)

        def chunk_before(b, p, s):
            if s % 2 or known(b, 1) or (s == 0 and known(b, 2)):
                return None
            return (b - 1, 1 - p, s // 2 - 1) if s else (b - 2, p, TC - 1)

        tail_scaled = [probs[:, 0, c, :] for c in range(TC)]
        tail_x = [probs[:, 0, TC + c, :] for c in range(TC)]
        tail_out = [probs[:, 1, TC + c, :] for c in range(TC)]
        tail_mix = probs[:, 1, 0:TC, :]
        tail_in = [sem(f"tail_in{c}") for c in range(TC)]
        tail_stored = [sem(f"tail_stored{c}") for c in range(TC)]
        tail_squared, tail_scaled_ready = sem("tail_squared"), sem("tail_scaled_ready")
        tail_mean, tail_rstd = sem("tail_mean"), sem("tail_rstd")
        tail_shifted, tail_summed = sem("tail_shifted"), sem("tail_summed")
        tail_mixed, tail_paired = sem("tail_mixed"), sem("tail_paired")
        dve_rotated = sem("dve_rotated")
        BY_POOL = 1
        ROTATED = {0: 3, 2: 4, 3: 5}
        ALL_TURNED = TILES * STEPS * B
        BEFORE = TC * (B - 1) - 2

        block = ctx.enter_context(nc.Block())

        @block.sync
        def _(sp):
            def load_unit(u, g):
                sp.wait_ge(scores, TILES * 2 * (u - 1))
                rows.load(sp, u, g)

            def load_v(b, p):
                if not known(b, 2):
                    sp.wait_ge(valued, STEPS * (b - 1))
                sp.dma_start(v_sb[:, p], scr["v"][b].rearrange("c p e -> p c e")).then_inc(v_in[p], 16)

            def load_mod(b, p):
                if not known(b, 2):
                    sp.wait_ge(summed, TC * (b - 1))
                sp.dma_start(mod[:, p], mod_scr[b].partition_broadcast(P)).then_inc(mod_in[p], 16)

            def load_x(b, c):
                if not (known(b, 1) and c < 2):
                    sp.wait_ge(rotated, TC * b + c - 1)
                sp.dma_start(x_s[:, c % 2], x[b, c * P:(c + 1) * P, :]).then_inc(x_in[c % 2], 16)

            def store(b, c):
                sp.wait_ge(rotated, TC * b + c + 1)
                sp.dma_start(out[b, c * P:(c + 1) * P, :], acc[:, c % 2]).then_inc(stored[c % 2], 16)

            def batch(b, p, first=False, last=False):
                for g in range(NG):
                    if not first:
                        load_x(b - 1, g)
                    if not (last and g >= NG - 2):
                        load_unit(NG * b + g + 2, g)
                    if g == 0 and not last:
                        load_v(b + 1, 1 - p)
                    if g == 1:
                        load_mod(b, p)
                    if g > 0 and not first and not (last and g == NG - 1):
                        store(b - 1, g - 1)
                    if g == 0 and not known(b, 2):
                        store(b - 2, TC - 1)

            load_v(0, 0)
            for j in range(4):
                sp.wait_ge(qk_stored[j], 16 * 4 * B)
            batch(0, 0, first=True)
            batch(1, 1)
            with sp.Fori(2, B - 3, 2) as b:
                batch(b, 0)
                batch(b + 1, 1)
            batch(B - 2, 0)
            batch(B - 1, 1, last=True)
            sp.wait_ge(turned, ALL_TURNED - TILES)
            for c in range(TC):
                sp.dma_start(tail_x[c], x[B - 1, c * P:(c + 1) * P, :]).then_inc(tail_in[c], 16)
            for c in (TC - 2, TC - 1):
                sp.wait_ge(dve_rotated, c - TC + 3)
                sp.dma_start(out[B - 2, c * P:(c + 1) * P, :], acc[:, c % 2]).then_inc(stored[c % 2], 16)
            for c in (0, 2, BY_POOL, 3):
                if c == BY_POOL:
                    sp.wait_ge(rotated, BEFORE + 1)
                else:
                    sp.wait_ge(dve_rotated, ROTATED[c])
                sp.dma_start(out[B - 1, c * P:(c + 1) * P, :], tail_out[c]).then_inc(tail_stored[c], 16)
            for j in range(2):
                sp.wait_ge(stored[j], 16 * TC * (B - 1) // 2)
            for c in range(TC):
                sp.wait_ge(tail_stored[c], 16)

        @block.tensor
        def _(pe):
            def score(b, s, r):
                n, g, half = STEPS * b + s, s // 2, s % 2
                p, i = g % 2, r // 2
                if r == 0 and half == 0:
                    seen = 32 * (NG * b + g - p) + 64
                    pe.wait_ge(rows.q_in[p], seen)
                    pe.wait_ge(rows.k_in[p], seen)
                if not (known(n, 1) and r < 4):
                    pe.wait_ge(masked, TILES * n + r - 3)
                c = 2 * half + r % 2
                pe.matmul(score_ps[:, r % 4, :], rows.q[:, p, i, c * P:(c + 1) * P], rows.k[:, p, i, :],
                          start=True, stop=True).then_inc(scores, 1)

            def turn(b, s, r):
                n = STEPS * b + s
                if r % 2 == 0:
                    pe.wait_ge(exped, TILES * n + r + 2)
                if not (known(n, 1) and r < 2):
                    if r < 2:
                        moved_out(pe, n - 1, TILES - 2 + r)
                    else:
                        moved_out(pe, n, r - 2)
                for j in range(2):
                    for c in range(2):
                        key = (2 * (r % 2) + j) * P
                        last = pe.transpose(prob_ps[:, r % 2, j * HALF + c * P:j * HALF + (c + 1) * P],
                                            probs[:, s % 2, r // 2 * 2 + c, key:key + P], ident[:, :])
                last.then_inc(turned, 1)

            def value(b, s, p, j):
                n, g = STEPS * b + s, s // 2
                if s == 0 and j == 0:
                    pe.wait_ge(v_in[p], 8 * (b - p) + 16)
                if j == 0:
                    pe.wait_ge(out_act, len(BY_ACT) * (n + 1))
                    pe.wait_ge(out_dve, len(BY_DVE) * (n + 1))
                    if not known(n, 1):
                        pe.wait_ge(raw_out, n)
                for i in range(HG):
                    h = HG * g + i
                    last = pe.matmul(value_ps[i * D:(i + 1) * D, :], v_sb[:, p, j, h * D:(h + 1) * D],
                                     probs_T[:, s % 2, i, j, :], start=(j == 0), stop=(j == TC - 1))
                if j == TC - 1:
                    last.then_inc(valued, 1)

            def turn_scale(n):
                pe.wait_ge(inverted, n + 1)
                if not known(n, 1):
                    pe.wait_ge(raw_out, n)
                for c in range(2):
                    last = pe.transpose(scale_ps[:, c * P:(c + 1) * P],
                                        inv_den[:, c].rearrange("p i d -> p (i d)"), ident[:, :])
                last.then_inc(scale_turned, 1)

            def project(b, p, c, k, y):
                if k == 0:
                    pe.wait_ge(o_ready, STEPS * b + STEPS - 1 + c // 2)
                    if y is y_ps and not (known(b, 1) and c == 0):
                        pe.wait_ge(scaled_ready, TC * b + c)
                t = slice(c * P, (c + 1) * P)
                pe.matmul(y[:, :], o_hi[:, p, k, t], wo_hi[:, k, :], start=(k == 0), stop=False)
                pe.matmul(y[:, :], o_hi[:, p, k, t], wo_lo[:, k, :], start=False, stop=False)
                last = pe.matmul(y[:, :], o_lo[:, p, k, t], wo_hi[:, k, :], start=False, stop=(k == KC - 1))
                if k == KC - 1:
                    last.then_inc(y_ready, 1)

            def batch(b, p, first=False, last=False):
                for s in range(STEPS):
                    n = STEPS * b + s
                    for r in range(TILES):
                        if tile_ahead(b, s, r + SCORE_AHEAD, last):
                            score(*tile_ahead(b, s, r + SCORE_AHEAD, last))
                        if r in PROJECT_AT and s % 2 == 1 and not first:
                            project(b - 1, 1 - p, s // 2, PROJECT_AT.index(r), y_ps)
                        if r in PROJECT_AT and chunk_before(b, p, s):
                            project(*chunk_before(b, p, s), 2 + PROJECT_AT.index(r), y_ps)
                        if r in VALUE_AT and s > 0:
                            value(b, s - 1, p, VALUE_AT.index(r))
                        if r in VALUE_AT and s == 0 and not first:
                            value(b - 1, STEPS - 1, 1 - p, VALUE_AT.index(r))
                        if r >= 1:
                            turn(b, s, r - 1)
                        if r == TURN_SCALE_AT and not (first and s == 0):
                            turn_scale(n - 1)
                    turn(b, s, TILES - 1)

            for r in range(TILES + SCORE_AHEAD):
                score(0, r // TILES, r % TILES)
            batch(0, 0, first=True)
            batch(1, 1)
            with pe.Fori(2, B - 3, 2) as b:
                batch(b, 0)
                batch(b + 1, 1)
            batch(B - 2, 0)
            batch(B - 1, 1, last=True)
            for k in (2, 3):
                project(B - 2, 0, TC - 1, k, y_ps)
            for j in range(TC):
                value(B - 1, STEPS - 1, 1, j)
            turn_scale(STEPS * B - 1)
            pe.wait_ge(masked, TILES * STEPS * B)
            for c in range(TC):
                for k in range(KC):
                    project(B - 1, 1, c, k, score_ps[:, c, :])

        @block.vector
        def _(dve):
            def mask(b, s, r):
                n = STEPS * b + s
                dve.wait_ge(scores, TILES * n + r + 1)
                if not known(n, 2):
                    dve.wait_ge(turned, TILES * (n - 2) + r // 2 * 2 + 2)
                take_waits(dve)
                c = 2 * (s % 2) + r % 2
                dve.tensor_tensor_reduce(probs[:, s % 2, r, :], score_ps[:, r % 4, :], mask_bias[:, c, :], 1.0, 3e38,
                                         ALU.add, ALU.min, least[:, s % 2, r:r + 1]).then_inc(masked, 1)

            def invert(n, s):
                dve.wait_ge(exped, TILES * (n + 1))
                if not known(n, 1):
                    dve.wait_ge(scale_turned, n)
                dve.reciprocal(inv_sum[:, :, :], den[:, s % 2].rearrange("p (i c) -> p c i", c=2)).then_inc(inv_sum_ready, 1)
                dve.wait_ge(inv_sum_ready, n + 1)
                dve.tensor_copy(inv_den[:, :, :, :], inv_sum[:, :, :].unsqueeze(3).to_broadcast([P, 2, HG, D])
                                ).then_inc(inverted, 1)

            def move_out(n, s, r):
                dve.wait_ge(turned, TILES * n + r + 1)
                if not known(n, 2):
                    dve.wait_ge(valued, n - 1)
                dve.tensor_copy(probs_T[:, s % 2, r // 2, 2 * (r % 2):2 * (r % 2) + 2, :],
                                prob_ps[:, r % 2, :].rearrange("p (j t) -> p j t", j=2)).then_inc(out_dve, 1)

            def rescale(b, p, c):
                m = TC * b + c
                if c == 0:
                    dve.wait_ge(mod_in[p], 8 * (b - p) + 16)
                dve.wait_ge(squared, m + 1)
                if not known(m, 1):
                    dve.wait_ge(summed, m)
                dve.tensor_tensor(scaled[:, :], y_ps[:, :], mod[:, p, E:], ALU.mult).then_inc(scaled_ready, 1)

            def residual(b, p, c):
                m = TC * b + c
                dve.wait_ge(scaled_ready, m + 1)
                dve.wait_ge(rstd_ready, m + 1)
                dve.wait_ge(shifted, m + 1)
                dve.scalar_tensor_tensor(x_s[:, c % 2], scaled[:, :], rstd[:, c % 2:c % 2 + 1], x_s[:, c % 2],
                                         ALU.mult, ALU.add).then_inc(summed, 1)

            def batch(b, p, first=False, last=False):
                for s in range(STEPS):
                    n = STEPS * b + s
                    for r in range(TILES):
                        if tile_ahead(b, s, r + MASK_AHEAD, last):
                            mask(*tile_ahead(b, s, r + MASK_AHEAD, last))
                        if r == INVERT_AT:
                            invert(n, s)
                        if r >= 1 and r - 1 in BY_DVE:
                            move_out(n, s, r - 1)
                        if r == RESCALE_AT and chunk_before(b, p, s):
                            rescale(*chunk_before(b, p, s))
                        if r == RESIDUAL_AT and s % 2 == 1 and chunk_before(b, p, s - 1):
                            residual(*chunk_before(b, p, s - 1))
                    if TILES - 1 in BY_DVE:
                        move_out(n, s, TILES - 1)

            for r in range(TILES + MASK_AHEAD):
                mask(0, r // TILES, r % TILES)
            batch(0, 0, first=True)
            batch(1, 1)
            with dve.Fori(2, B - 3, 2) as b:
                batch(b, 0)
                batch(b + 1, 1)
            batch(B - 2, 0)
            batch(B - 1, 1, last=True)
            rescale(B - 2, 0, TC - 1)
            def rotate(i, chunk, to):
                dve.wait_ge(turned, ALL_TURNED)
                if i > 0:
                    dve.wait_ge(dve_rotated, i)
                rotation_products(dve, tail_mix, chunk).then_inc(tail_mixed, 1)
                dve.wait_ge(tail_mixed, i + 1)
                dve.tensor_tensor(tail_mix[:, 0:2, :], tail_mix[:, 0:2, :], tail_mix[:, 2:4, :],
                                  ALU.add).then_inc(tail_paired, 1)
                dve.wait_ge(tail_paired, i + 1)
                dve.tensor_tensor(to, tail_mix[:, 0, :], tail_mix[:, 1, :], ALU.add).then_inc(dve_rotated, 1)

            def tail_rescale(c):
                dve.wait_ge(tail_squared, c + 1)
                dve.tensor_tensor(tail_scaled[c], score_ps[:, c, :], mod[:, 1, E:], ALU.mult).then_inc(tail_scaled_ready, 1)

            def tail_residual(c):
                dve.wait_ge(tail_rstd, c // 2 + 1)
                dve.wait_ge(tail_shifted, c + 1)
                dve.scalar_tensor_tensor(tail_x[c], tail_scaled[c], tail_inv_rms[:, c:c + 1], tail_x[c],
                                         ALU.mult, ALU.add).then_inc(tail_summed, 1)

            for c in (TC - 2, TC - 1):
                if c == TC - 1:
                    residual(B - 2, 0, c)
                dve.wait_ge(summed, TC * (B - 2) + c + 1)
                dve.wait_ge(stored[c % 2], 16 * (TC * (B - 1) // 2 - 1))
                rotate(c - TC + 2, x_s[:, c % 2], acc[:, c % 2])
            for c in (0, 1):
                tail_rescale(c)
            dve.wait_ge(tail_scaled_ready, 2)
            for c in (1, 0):
                tail_residual(c)
            dve.wait_ge(tail_summed, 2)
            rotate(2, tail_x[0], tail_out[0])
            for c in (2, 3):
                tail_rescale(c)
            dve.wait_ge(tail_scaled_ready, 4)
            for c in (2, 3):
                tail_residual(c)
            dve.wait_ge(tail_summed, 4)
            for c in (2, 3):
                rotate(c + 1, tail_x[c], tail_out[c])

        @block.scalar
        def _(act):
            def exp(n, s, r):
                act.wait_ge(masked, TILES * n + r + 1)
                if r == 0 and not known(n, 2):
                    act.wait_ge(inverted, n - 1)
                act.activation(probs[:, s % 2, r, :], probs[:, s % 2, r, :], ACT.Exp, bias=least[:, s % 2, r:r + 1],
                               scale=-1.0, accum_out=den[:, s % 2, r:r + 1]).then_inc(exped, 1)

            def move_out(n, s, r):
                act.wait_ge(turned, TILES * n + r + 1)
                if not known(n, 2):
                    act.wait_ge(valued, n - 1)
                act.activation(probs_T[:, s % 2, r // 2, 2 * (r % 2):2 * (r % 2) + 2, :],
                               prob_ps[:, r % 2, :].rearrange("p (j t) -> p j t", j=2), ACT.Copy).then_inc(out_act, 1)

            def values_out(n, s):
                act.wait_ge(valued, n + 1)
                act.wait_ge(scale_turned, n + 1)
                if not known(n, 2):
                    act.wait_ge(o_scaled, n - 1)
                act.activation(raw_T[:, s % 2], out_ps[:, :, :], ACT.Copy).then_inc(raw_out, 1)

            def square(b, p, c):
                m = TC * b + c
                act.wait_ge(y_ready, m + 1)
                if not known(m, 1):
                    act.wait_ge(squared, m)
                if not known(m, 2):
                    act.wait_ge(mean_ready, m - 1)
                act.activation(junk[:, :], y_ps[:, :], ACT.Square,
                               accum_out=sum_sq[:, c % 2:c % 2 + 1]).then_inc(squared, 1)

            def batch(b, p, first=False, last=False):
                for s in range(STEPS):
                    n = STEPS * b + s
                    for r in range(TILES):
                        if not (last and s == STEPS - 1):
                            exp(n + 1, s + 1, r)
                        if r >= 1 and r - 1 in BY_ACT:
                            move_out(n, s, r - 1)
                        if r == VALUES_OUT_AT and not (first and s == 0):
                            values_out(n - 1, s - 1)
                        if r == SQUARE_AT and chunk_before(b, p, s):
                            square(*chunk_before(b, p, s))
                    if TILES - 1 in BY_ACT:
                        move_out(n, s, TILES - 1)

            for r in range(TILES):
                exp(0, 0, r)
            batch(0, 0, first=True)
            batch(1, 1)
            with act.Fori(2, B - 3, 2) as b:
                batch(b, 0)
                batch(b + 1, 1)
            batch(B - 2, 0)
            batch(B - 1, 1, last=True)
            square(B - 2, 0, TC - 1)
            values_out(STEPS * B - 1, STEPS - 1)
            for c in range(TC):
                act.wait_ge(y_ready, TC * (B - 1) + c + 1)
                if c == 0:
                    act.wait_ge(squared, TC * (B - 1))
                else:
                    act.wait_ge(tail_squared, c)
                act.activation(junk[:, :], score_ps[:, c, :], ACT.Square,
                               accum_out=tail_sum_sq[:, c:c + 1]).then_inc(tail_squared, 1)

        @block.gpsimd
        def _(pool):
            def split(b, p, s):
                n = STEPS * b + s
                g, half = s // 2, s % 2
                t = slice(half * HALF, (half + 1) * HALF)
                if s == 0 and not known(b, 2):
                    pool.wait_ge(y_ready, TC * (b - 1))
                pool.wait_ge(raw_out, n + 1)
                if not known(n, 2):
                    pool.wait_ge(o_ready, n - 1)
                pool.tensor_tensor(o_T[:, s % 2], raw_T[:, s % 2, 0], raw_T[:, s % 2, 1], ALU.mult).then_inc(o_scaled, 1)
                pool.wait_ge(o_scaled, n + 1)
                take_waits(pool)
                pool.tensor_copy(o_hi[:, p, g, t], o_T[:, s % 2]).then_inc(o_hi_ready, 1)
                pool.wait_ge(o_hi_ready, n + 1)
                pool.tensor_tensor(o_lo[:, p, g, t], o_T[:, s % 2], f32(o_hi[:, p, g, t]),
                                   ALU.subtract).then_inc(o_ready, 1)

            def shift(b, p, c):
                m = TC * b + c
                if c == 0:
                    pool.wait_ge(mod_in[p], 8 * (b - p) + 16)
                pool.wait_ge(x_in[c % 2], 16 * (2 * b + c // 2 + 1))
                pool.tensor_tensor(x_s[:, c % 2], x_s[:, c % 2], mod[:, p, 0:E], ALU.add).then_inc(shifted, 1)

            def rms(b, p, c):
                m = TC * b + c
                pool.wait_ge(squared, m + 1)
                take_waits(pool)
                pool.tensor_scalar(mean_sq[:, c % 2:c % 2 + 1], sum_sq[:, c % 2:c % 2 + 1], 1.0 / E, RMS_EPS,
                                   ALU.mult, ALU.add).then_inc(mean_ready, 1)
                pool.wait_ge(mean_ready, m + 1)
                if not known(m, 2):
                    pool.wait_ge(summed, m - 1)
                pool.tensor_tensor(rstd[:, c % 2:c % 2 + 1], mean_sq[:, c % 2:c % 2 + 1], neg_half[:, :],
                                   ALU.pow).then_inc(rstd_ready, 1)

            def rotate(b, p, c):
                m = TC * b + c
                pool.wait_ge(summed, m + 1)
                if not known(m, 2):
                    pool.wait_ge(stored[c % 2], 16 * (2 * b + c // 2))
                if not known(m, 1):
                    pool.wait_ge(rotated, m)
                rotation_products(pool, mix, x_s[:, c % 2]).then_inc(mixing, 1)
                pool.wait_ge(mixing, m + 1)
                pool.tensor_tensor(mix[:, 0:2, :], mix[:, 0:2, :], mix[:, 2:4, :], ALU.add).then_inc(paired, 1)
                pool.wait_ge(paired, m + 1)
                pool.tensor_tensor(acc[:, c % 2], mix[:, 0, :], mix[:, 1, :], ALU.add).then_inc(rotated, 1)

            def batch(b, p, first=False, last=False):
                for s in range(STEPS):
                    if s % 2 == 0 and not first:
                        shift(b - 1, 1 - p, s // 2)
                    if chunk_before(b, p, s):
                        rms(*chunk_before(b, p, s))
                    if s % 2 == 1 and chunk_before(b, p, s - 1) and not (last and s == STEPS - 1):
                        rotate(*chunk_before(b, p, s - 1))
                    if s > 0:
                        split(b, p, s - 1)
                    elif not first:
                        split(b - 1, 1 - p, STEPS - 1)

            pool.memset(neg_half[:, :], -0.5).then_inc(half_set, 1)
            pool.wait_ge(half_set, 1)
            batch(0, 0, first=True)
            batch(1, 1)
            with pool.Fori(2, B - 3, 2) as b:
                batch(b, 0)
                batch(b + 1, 1)
            batch(B - 2, 0)
            batch(B - 1, 1, last=True)
            rms(B - 2, 0, TC - 1)
            split(B - 1, 1, STEPS - 1)
            pool.wait_ge(mod_in[1], 16 * (B // 2))
            for pair in range(2):
                for c in (2 * pair, 2 * pair + 1):
                    pool.wait_ge(tail_in[c], 16)
                    pool.tensor_tensor(tail_x[c], tail_x[c], mod[:, 1, 0:E], ALU.add).then_inc(tail_shifted, 1)
                cols = slice(2 * pair, 2 * pair + 2)
                pool.wait_ge(tail_squared, 2 * pair + 2)
                pool.tensor_scalar(tail_mean_sq[:, cols], tail_sum_sq[:, cols], 1.0 / E, RMS_EPS,
                                   ALU.mult, ALU.add).then_inc(tail_mean, 1)
                pool.wait_ge(tail_mean, pair + 1)
                pool.tensor_tensor(tail_inv_rms[:, cols], tail_mean_sq[:, cols],
                                   neg_half[:, :].to_broadcast([P, 2]), ALU.pow).then_inc(tail_rstd, 1)
            pool.wait_ge(tail_summed, 1)
            pool.wait_ge(rotated, BEFORE)
            rotation_products(pool, mix, tail_x[BY_POOL]).then_inc(mixing, 1)
            pool.wait_ge(mixing, BEFORE + 1)
            pool.tensor_tensor(mix[:, 0:2, :], mix[:, 0:2, :], mix[:, 2:4, :], ALU.add).then_inc(paired, 1)
            pool.wait_ge(paired, BEFORE + 1)
            pool.wait_ge(turned, ALL_TURNED)
            pool.tensor_tensor(tail_out[BY_POOL], mix[:, 0, :], mix[:, 1, :], ALU.add).then_inc(rotated, 1)


def program(nc, x, xT, cond, condT, mask, wT, rms_scale, wcT, bc, q_right, gate, out):
    scr = {n: nc.dram_tensor(f"{n}_scratch", (B * NG, 2, P, S), F32, kind="Internal").ap() for n in "qk"}
    scr["v"] = nc.dram_tensor("v_scratch", (B, TC, P, E), F32, kind="Internal").ap()
    mod_scr = nc.dram_tensor("mod_scratch", (B, 2 * E), F32, kind="Internal").ap()
    with ExitStack() as ctx:
        wo_hi = ctx.enter_context(nc.sbuf_tensor("wo_hi", [P, KC, E], F32R))
        wo_lo = ctx.enter_context(nc.sbuf_tensor("wo_lo", [P, KC, E], F32R))
        mask_bias = ctx.enter_context(nc.sbuf_tensor("mask_bias", [P, TC, S], BF16))
        rot = ctx.enter_context(nc.sbuf_tensor("rot", [P, 4, 4, C], F32))
        ident = ctx.enter_context(nc.sbuf_tensor("ident", [P, P], F32))
        with nc.sbuf_tensor("raw", [P, 4, KC, S], F32) as raw:
            pass
        rows = Rows(nc, ctx, scr)
        late = ctx.enter_context(nc.sbuf_tensor("late", [P, 8, 512], F32))
        qk_stored = [ctx.enter_context(nc.semaphore(f"qk_stored{i}")) for i in range(4)]
        projections(nc, xT, wT, scr, raw, rows, late, qk_stored, wo_hi, wo_lo, mask, condT, cond, wcT, bc, rms_scale,
                    q_right, gate, mod_scr, mask_bias, rot, ident)
        attention(nc, x, scr, rows, late, qk_stored, mod_scr, out, mask_bias, rot, ident, wo_hi, wo_lo)


def kernel(**inputs):
    import numpy as np
    import concourse.bacc as bacc
    from concourse.bass_utils import run_bass_kernel_spmd

    def laid(a):
        return np.ascontiguousarray(a)

    nc = bacc.Bacc("TRN2", target_bir_lowering=False, num_devices=1)
    x, cond = np.asarray(inputs["x"]), np.asarray(inputs["cond_256"])
    arrays = {
        "x": laid(x),
        "xT": laid(x.transpose(0, 2, 1)),
        "cond": laid(cond.reshape(-1)),
        "condT": laid(cond.T),
        "mask": laid(np.asarray(inputs["mask_SxS_bk1"]).view(np.int32)),
        "wqT": laid(np.asarray(inputs["L0_cond_Wq"]).T),
        "wkT": laid(np.asarray(inputs["L0_cond_Wk"]).T),
        "wvT": laid(np.asarray(inputs["L0_cond_Wv"]).T),
        "woT": laid(np.asarray(inputs["L0_cond_Wo"]).T),
        "rms_scale": laid(inputs["L0_cond_rms_scale"]),
        "wcT": laid(np.asarray(inputs["L0_cond_Wc"]).T),
        "bc": laid(inputs["L0_cond_bc"]),
        "q_right": laid(np.asarray(inputs["L1_cond_q_right"]).reshape(-1)),
        "gate": laid(np.asarray(inputs["L1_cond_spectral_gate"]).reshape(-1)),
    }
    dram = {n: nc.dram_tensor(f"in_{n}", a.shape, mybir.dt.from_np(a.dtype), kind="ExternalInput").ap()
            for n, a in arrays.items()}
    out = nc.dram_tensor("out_0", (B, S, E), F32, kind="ExternalOutput").ap()
    program(nc, dram["x"], dram["xT"], dram["cond"], dram["condT"], dram["mask"],
            [dram["wqT"], dram["wkT"], dram["wvT"], dram["woT"]], dram["rms_scale"], dram["wcT"], dram["bc"],
            dram["q_right"], dram["gate"], out)
    r = run_bass_kernel_spmd(nc, [{f"in_{n}": a for n, a in arrays.items()}], core_ids=[0])
    return r.results[0]["out_0"]
```
